# Optimizing a Trainium2 kernel written in Bass

```python
import numpy as np
import jax
import jax.numpy as jnp

def _softmax(x, axis=-1):
    return jax.nn.softmax(x, axis=axis)

def _gelu(x):
    return jax.nn.gelu(x, approximate=True)

def _silu(x):
    return jax.nn.silu(x)

def _sigmoid(x):
    return jax.nn.sigmoid(x)

def _layernorm(x, axis=-1, eps=1e-05):
    m = jnp.mean(x, axis=axis, keepdims=True)
    v = jnp.var(x, axis=axis, keepdims=True)
    return (x - m) / jnp.sqrt(v + eps)

def _scatter_add(tgt, idx, src, axis=0):
    return tgt.at[idx].add(src)

def _segment_sum(src, seg, n):
    return jax.ops.segment_sum(src, seg, n)
kernel_name = 'mk_seq_postln_d1_jaxref_r8_59decb'

def setup_inputs(seed: int=0):
    np.random.seed(seed)
    _w = jnp.asarray

    def _L0_attn_setup():
        import jax, jax.numpy as jnp
        import numpy as np
        B, T, D = (2, 256, 512)
        H, KVH = (32, 8)
        HD = D // H
        key = jax.random.key(seed)
        ks = jax.random.split(key, 5)
        s = 0.02
        return {'x': jax.random.normal(ks[0], (B, T, D), dtype=jnp.float32), 'Wq': jax.random.normal(ks[1], (D, D), dtype=jnp.float32) * s, 'bq': jnp.zeros((D,), dtype=jnp.float32), 'Wk': jax.random.normal(ks[2], (D, KVH * HD), dtype=jnp.float32) * s, 'bk': jnp.zeros((KVH * HD,), dtype=jnp.float32), 'Wv': jax.random.normal(ks[3], (D, KVH * HD), dtype=jnp.float32) * s, 'bv': jnp.zeros((KVH * HD,), dtype=jnp.float32), 'Wo': jax.random.normal(ks[4], (D, D), dtype=jnp.float32) * s, 'bo': jnp.zeros((D,), dtype=jnp.float32)}
    _L0_attn_in = _L0_attn_setup()

    def _L0_ffn_setup():
        import jax, jax.numpy as jnp
        import numpy as np
        HIDDEN = 512
        INTER = 1376

        def _ternary_quantize(w):
            scale = jnp.mean(jnp.abs(w))
            return jnp.clip(jnp.round(w / scale), -1.0, 1.0) * scale
        key = jax.random.key(seed)
        kx, kg, ku, kd = jax.random.split(key, 4)
        x = jax.random.normal(kx, (2, 256, HIDDEN), dtype=jnp.float32)
        w_gate = _ternary_quantize(jax.random.normal(kg, (INTER, HIDDEN), dtype=jnp.float32) * 0.02)
        w_up = _ternary_quantize(jax.random.normal(ku, (INTER, HIDDEN), dtype=jnp.float32) * 0.02)
        w_down = _ternary_quantize(jax.random.normal(kd, (HIDDEN, INTER), dtype=jnp.float32) * 0.02)
        return {'x': x, 'w_gate': w_gate, 'w_up': w_up, 'w_down': w_down}
    _L0_ffn_in = _L0_ffn_setup()
    _d = {'L0_attn_x': _L0_attn_in['x'], 'L0_attn_Wq': _L0_attn_in['Wq'], 'L0_attn_bq': _L0_attn_in['bq'], 'L0_attn_Wk': _L0_attn_in['Wk'], 'L0_attn_bk': _L0_attn_in['bk'], 'L0_attn_Wv': _L0_attn_in['Wv'], 'L0_attn_bv': _L0_attn_in['bv'], 'L0_attn_Wo': _L0_attn_in['Wo'], 'L0_attn_bo': _L0_attn_in['bo'], 'L0_ffn_w_gate': _L0_ffn_in['w_gate'], 'L0_ffn_w_up': _L0_ffn_in['w_up'], 'L0_ffn_w_down': _L0_ffn_in['w_down']}
    _x0 = _d['L0_attn_x']
    _d['L0_attn_x'] = jax.random.normal(jax.random.fold_in(jax.random.key(seed), 1), (4, 256, 512), dtype=_x0.dtype)
    del _x0
    return _d

def reference(L0_attn_x, L0_attn_Wq, L0_attn_bq, L0_attn_Wk, L0_attn_bk, L0_attn_Wv, L0_attn_bv, L0_attn_Wo, L0_attn_bo, L0_ffn_w_gate, L0_ffn_w_up, L0_ffn_w_down):

    def _L0_attn_ref(x, Wq, bq, Wk, bk, Wv, bv, Wo, bo):
        import jax, jax.numpy as jnp
        import numpy as np
        B, T, D = (2, 256, 512)
        H, KVH = (32, 8)
        HD = D // H
        b, t, d = x.shape
        h, kvh = (H, KVH)
        hd = d // h
        q = (x @ Wq + bq).reshape(b, t, h, hd).transpose(0, 2, 1, 3)
        k = (x @ Wk + bk).reshape(b, t, kvh, hd).transpose(0, 2, 1, 3)
        v = (x @ Wv + bv).reshape(b, t, kvh, hd).transpose(0, 2, 1, 3)
        rep = h // kvh
        k = jnp.repeat(k, rep, axis=1)
        v = jnp.repeat(v, rep, axis=1)
        scale = 1.0 / np.sqrt(hd).astype(np.float32)
        scores = jnp.einsum('bhqd,bhkd->bhqk', q, k) * scale
        mask = jnp.triu(jnp.full((t, t), -jnp.inf, dtype=scores.dtype), k=1)
        scores = scores + mask
        attn = jax.nn.softmax(scores, axis=-1)
        out = jnp.einsum('bhqk,bhkd->bhqd', attn, v)
        out = out.transpose(0, 2, 1, 3).reshape(b, t, d)
        out = out @ Wo + bo
        return out

    def _L0_ffn_ref(x, w_gate, w_up, w_down):
        import jax, jax.numpy as jnp
        import numpy as np
        HIDDEN = 512
        INTER = 1376

        def _ternary_quantize(w):
            scale = jnp.mean(jnp.abs(w))
            return jnp.clip(jnp.round(w / scale), -1.0, 1.0) * scale
        xf = x.astype(jnp.float32) / 128.0
        gate = jnp.einsum('bsh,ih->bsi', xf, w_gate)
        up = jnp.einsum('bsh,ih->bsi', xf, w_up)
        inter = jax.nn.silu(gate) * up
        inter_q = jnp.trunc(jnp.clip(inter * 128.0, -128.0, 127.0)).astype(jnp.int8)
        down = jnp.einsum('bsi,hi->bsh', inter_q.astype(jnp.float32), w_down)
        out = jnp.trunc(jnp.clip(down * 128.0, -128.0, 127.0)).astype(jnp.int8)
        return out
    x = L0_attn_x
    x = _layernorm(x + _L0_attn_ref(x, L0_attn_Wq, L0_attn_bq, L0_attn_Wk, L0_attn_bk, L0_attn_Wv, L0_attn_bv, L0_attn_Wo, L0_attn_bo), axis=-1)
    x = _layernorm(x + _L0_ffn_ref(x, L0_ffn_w_gate, L0_ffn_w_up, L0_ffn_w_down), axis=-1)
    return x

_drawn_inputs = setup_inputs


def setup_inputs(seed=0):
    import zlib

    import numpy as np

    out = dict(_drawn_inputs(seed))
    spreads = {'L0_attn_bq': (0.0, 0.8),
     'L0_attn_bk': (0.0, 0.8),
     'L0_attn_bv': (0.0, 0.1),
     'L0_attn_bo': (0.0, 0.1)}
    factors = {'L0_attn_Wq': 8.0, 'L0_attn_Wk': 8.0}
    for name, (base, spread) in spreads.items():
        noise = np.random.default_rng([zlib.crc32(name.encode()), seed]).standard_normal(out[name].shape)
        drawn = base * np.exp(spread * noise) if base else spread * noise
        out[name] = jnp.asarray(drawn.astype(out[name].dtype))
    for name, factor in factors.items():
        out[name] = (out[name] * factor).astype(out[name].dtype)
    return out
```

```python
from contextlib import ExitStack

import concourse.bass as bass
from concourse import mybir

ALU = mybir.AluOpType
ACT = mybir.ActivationFunctionType
AX = mybir.AxisListType
F32 = mybir.dt.float32
F32R = mybir.dt.float32r
BF16 = mybir.dt.bfloat16
I16 = mybir.dt.int16
I32 = mybir.dt.int32

P = 128
BANK = 512
LN_EPS = 1e-5
MASKED = -1e30
ROUND_TO_INT = 1.5 * 2.0 ** 23
TRUNC_OFFSET = 0.5 - 2.0 ** -13
ABS_12_BITS = 0x7FFFF000


def layer(nc, xT, x_tok, w_qkv, b_qkv, w_o, b_o, w_gate_up, w_down, out):
    D, N = xT.shape
    T = 256
    HD = 16
    H = D // HD
    KV = (w_qkv.shape[1] - D) // 2 // HD
    REP = H // KV
    NB = N // T
    TT = N // P
    C = D // P
    I_TILES = w_down.shape[0]
    HALF = N // 2
    TTH = TT // 2
    STEPS = NB * KV
    SH = STEPS // 2
    UNIT = 4
    UH = UNIT * REP
    KVD = KV * HD
    QKV = D + 2 * KVD
    W4 = 4 * HD
    EXTRA = 3 * HD
    LAG2, LAGV, LAGT = 6, 7, 8
    SCALE = float(HD) ** -0.5
    assert REP == 4 and C == 4 and T == 2 * P and QKV == 768

    ctx = ExitStack()
    with ctx:
        def keep(name, shape, dt):
            return ctx.enter_context(nc.sbuf_tensor(name, shape, dt))

        def sem(name):
            return ctx.enter_context(nc.semaphore(name))

        bank = [ctx.enter_context(nc.psum_tensor(f"bank{i}", [P, BANK], F32)) for i in range(8)]

        identity = keep("identity", [P, P], F32)
        identity_bf = keep("identity_bf", [P, P], BF16)
        later_keys = keep("later_keys", [P, REP, P], BF16)
        bo_rows = keep("bo_rows", [P, D], F32)
        stats = keep("stats", [P, 6], F32)
        mean_var = keep("mean_var", [P, 2, 2], F32)
        std = keep("std", [P, 2], F32)
        rstd = keep("rstd", [P, 2], F32)
        eps_col = keep("eps_col", [P, 1], F32)

        def in_turn(stack):
            return lambda name, shape, dt: stack.enter_context(nc.sbuf_tensor(name, shape, dt))

        with ExitStack() as first:
            sb = in_turn(first)
            o_tok = sb("o_tok", [P, TT, D], F32)
            with ExitStack() as attention:
                sb = in_turn(attention)
                wh = sb("wqkv_hi", [P, C, QKV], F32R)
                wl = sb("wqkv_lo", [P, C, QKV], F32R)
                xh = sb("xT_hi", [P, C, HALF], F32R)
                xl = sb("xT_lo", [P, C, HALF], F32R)
                qkv_rows = sb("qkv_rows", [P, 2, QKV], F32)
                q_stack = sb("q_stack", [P, 2, H, W4], F32)
                k_stack = sb("k_stack", [P, 2, KV, 2 * W4], F32)
                bqkv_rows = sb("bqkv_rows", [P, QKV], F32)
                QT = sb("QT", [P, H // 2, HALF], F32R)
                KTe = sb("KTe", [P, KV, HALF], F32R)
                KTo = sb("KTo", [P, KV, HALF], F32R)
                v_ones = sb("v_ones", [P, TT, KV, 2 * HD], F32)
                probs = sb("probs", [P, 2, 3, REP, P], F32)
                neg_max = sb("neg_max", [P, 2, 2, UH], F32)
                max_rows = sb("max_rows", [UH, 2, 2, T], F32R)
                o_cols = sb("o_cols", [P, 2, T], F32)
                inv_sum = sb("inv_sum", [P, 2, REP], F32)
                w_raw = sb("wqkv_raw", [P, C, QKV], F32)
                x_raw = sb("xT_raw", [P, C, HALF], F32)
            with ExitStack() as projection:
                sb = in_turn(projection)
                wo_raw = sb("wo_raw", [P, C, D], F32)
                woh = sb("wo_hi", [P, C, D], F32R)
                wol = sb("wo_lo", [P, C, D], F32R)
        with ExitStack() as ffn:
            sb = in_turn(ffn)
            wdh = sb("w_down_hi", [P, I_TILES, D], F32R)
            wdl = sb("w_down_lo", [P, I_TILES, D], F32R)
            x1 = sb("x1", [P, TT, D], F32)
            gu_raw = sb("gate_up_raw", [P, 2, 2, C, P], F32)
            wd_raw = sb("w_down_raw", [P, 2, D], F32)
            guh = sb("gate_up_hi", [P, 2, 2, C, P], F32R)
            gul = sb("gate_up_lo", [P, 2, 2, C, P], F32R)
            oh = sb("oT_hi", [P, 2, C, P], F32R)
            ol = sb("oT_lo", [P, 2, C, P], F32R)
            y = sb("y", [P, 2, D], F32)
            x1h = sb("x1T_hi", [P, C, N], F32R)
            x1l = sb("x1T_lo", [P, C, N], F32R)
            inter_q = sb("inter_q", [P, I_TILES, N], BF16)
            inter_r = sb("inter_r", [P, 2, I_TILES, P], F32R)
            silu_g = sb("silu_g", [P, 2, BANK], F32)
            val = sb("val", [P, 2, BANK], F32)
            mag = sb("mag", [P, 2, BANK], F32)
            floor_mag = sb("floor_mag", [P, 2, BANK], I16)
            sign = sb("sign", [P, 2, BANK], BF16)
            q_int = sb("q_int", [P, 2, BANK], BF16)

        w_in = [sem(f"w_in{c}") for c in range(C)]
        x_in = [sem(f"x_in{c}") for c in range(C)]
        x2_in, bias_in, max_in, wo_in, x1_in = sem("x2_in"), sem("bias_in"), sem("max_in"), sem("wo_in"), sem("x1_in")
        raw_in = [sem("raw_in0"), sem("raw_in1")]
        stored = [sem("stored0"), sem("stored1")]
        consts, zeroed = sem("consts"), sem("zeroed")
        w_hi, w_lo, x_hi, x_lo = sem("w_hi"), sem("w_lo"), sem("x_hi"), sem("x_lo")
        q_done, kv_done = sem("q_done"), sem("kv_done")
        q_biased, kv_biased = sem("q_biased"), sem("kv_biased")
        q_hi, k_hi, q_lo, k_lo, v_in = sem("q_hi"), sem("k_hi"), sem("q_lo"), sem("k_lo"), sem("v_in")
        stack_t = sem("stack_t")
        t_act, t_dve = sem("t_act"), sem("t_dve")
        s0_done, s1_done, max0, max1 = sem("s0_done"), sem("s1_done"), sem("max0"), sem("max1")
        max_t, max_hi, max_lo = sem("max_t"), sem("max_hi"), sem("max_lo")
        st_done, exp_done, causal, pv_done = sem("st_done"), sem("exp_done"), sem("causal"), sem("pv_done")
        o_out, o_t, sum_inv, o_norm = sem("o_out"), sem("o_t"), sem("sum_inv"), sem("o_norm")
        wo_hi, wo_lo, x_bo = sem("wo_hi_s"), sem("wo_lo_s"), sem("x_bo")
        ot_done, ot_hi, ot_lo, wo_done = sem("ot_done"), sem("ot_hi"), sem("ot_lo"), sem("wo_done")
        y_done, var_done, std_done, x1_done = sem("y_done"), sem("var_done"), sem("std_done"), sem("x1_done")
        x1_t, x1_hi, x1_lo = sem("x1_t"), sem("x1_hi"), sem("x1_lo")
        gu_hi, gu_lo, wd_hi, wd_lo = sem("gu_hi"), sem("gu_lo"), sem("wd_hi"), sem("wd_lo")
        gate_done, up_done, silu_done, val_done = sem("gate_done"), sem("up_done"), sem("silu_done"), sem("val_done")
        sign_done, inter_done, inter_cast = sem("sign_done"), sem("inter_done"), sem("inter_cast")
        down_done, dval_done, dsign_done = sem("down_done"), sem("dval_done"), sem("dsign_done")
        var2_done, std2_done, out_done = sem("var2_done"), sem("std2_done"), sem("out_done")
        dve_step = sem("dve_step")

        STEPS_ALL = STEPS
        TR = H // 2 // 4 + KV // 4

        def at(s):
            return s // KV, s % KV, s // KV % (NB // 2)

        PAIRED = (I_TILES - 1) // 2

        def out_of_bank(copy, n, j, tok, done):
            src = bank[4 + n % 4][:, :].rearrange("p (k q) -> p k q", k=4)
            if j < H // 8:
                copy(QT[:, 4 * j:4 * j + 4, tok], src).then_inc(done, 1)
            else:
                g = 4 * (j - H // 8)
                copy(KTe[0:W4, g:g + 4, tok], src[0:W4])
                copy(KTo[W4:P, g:g + 4, tok], src[W4:P]).then_inc(done, 1)

        block = ctx.enter_context(nc.Block())

        @block.sync
        def _(sp):
            for c in range(C):
                sp.dma_start(w_raw[:, c, :], w_qkv[c * P:(c + 1) * P, :]).then_inc(w_in[c], 16)
                sp.dma_start(x_raw[:, c, :], xT[c * P:(c + 1) * P, 0:HALF]).then_inc(x_in[c], 16)
            sp.dma_start(bqkv_rows[:, :], b_qkv.partition_broadcast(P)).then_inc(bias_in, 16)
            sp.dma_start(bo_rows[:, :], b_o.partition_broadcast(P)).then_inc(bias_in, 16)
            sp.wait_ge(x_lo, C)
            sp.wait_ge(x_hi, C)
            sp.dma_start(x_raw[:, :, :], xT[:, HALF:N].rearrange("(c p) n -> p c n", p=P)).then_inc(x2_in, 16)

            def maxima(u):
                b, g0 = u * UNIT // KV, u * UNIT % KV
                cols = slice(b % 2 * T, b % 2 * T + T)
                sp.wait_ge(max_lo, u + 1)
                sp.wait_ge(max_hi, u + 1)
                for j in range(2):
                    for r in range(2):
                        row = W4 * j + EXTRA + r
                        sp.dma_start(QT[row:row + 1, 2 * g0:2 * g0 + UH // 2, cols].bitcast(F32),
                                     max_rows[j:UH:2, u % 2, r, :].bitcast(F32)).then_inc(max_in, 16)

            for u in range(SH // UNIT):
                maxima(u)
            sp.wait_ge(stack_t, TR * TT)
            sp.dma_start(wo_raw[:, :, :], w_o.rearrange("(c p) n -> p c n", p=P)).then_inc(wo_in, 16)
            sp.dma_start(x1[:, :, :], x_tok.rearrange("(t p) d -> p t d", p=P)).then_inc(x1_in, 16)

            def weights(t, slot):
                sp.dma_start(gu_raw[:, slot], w_gate_up[t]).then_inc(raw_in[slot], 16)
                sp.dma_start(wd_raw[:, slot], w_down[t]).then_inc(raw_in[slot], 16)

            weights(0, 0)
            weights(1, 1)
            for u in range(SH // UNIT, 2 * SH // UNIT):
                maxima(u)
            with sp.Fori(1, PAIRED) as i:
                for k in range(2):
                    for split in (gu_hi, gu_lo, wd_hi, wd_lo):
                        sp.wait_ge(split, 2 * i + (k - 1))
                    weights(2 * i + k, k)
            for split in (gu_hi, gu_lo, wd_hi, wd_lo):
                sp.wait_ge(split, I_TILES - 2)
            weights(I_TILES - 1, 0)
            for tt in range(TT):
                sp.wait_ge(out_done, tt + 1)
                sp.dma_start(out[tt * P:(tt + 1) * P, :], y[:, tt % 2, :]).then_inc(stored[tt % 2], 16)
            for k in range(2):
                sp.wait_ge(stored[k], 16 * TT // 2)

        @block.gpsimd
        def _(pool):
            nc.gpsimd.memset(identity[:, :], 0.0).then_inc(zeroed, 1)
            nc.gpsimd.memset(identity_bf[:, :], 0.0).then_inc(zeroed, 1)
            nc.gpsimd.memset(later_keys[:, :, :], 0.0).then_inc(zeroed, 1)
            pool.wait_ge(zeroed, 3)
            for m in (identity, identity_bf):
                nc.gpsimd.affine_select(out=m[:, :], in_=m[:, :], compare_op=ALU.not_equal, fill=1.0, base=0,
                                        pattern=[[-1, P]], channel_multiplier=1).then_inc(consts, 1)
            nc.gpsimd.affine_select(out=later_keys[:, :, :], in_=later_keys[:, :, :], compare_op=ALU.is_ge,
                                    fill=MASKED, base=0, pattern=[[0, REP], [-1, P]],
                                    channel_multiplier=1).then_inc(consts, 1)
            nc.gpsimd.memset(q_stack[:, :, :, EXTRA:W4], 0.0).then_inc(consts, 1)
            for j in range(2):
                nc.gpsimd.memset(k_stack[:, :, :, W4 * j + EXTRA:W4 * j + EXTRA + 2], 1.0).then_inc(consts, 1)
                nc.gpsimd.memset(k_stack[:, :, :, W4 * j + EXTRA + 2:W4 * (j + 1)], 0.0).then_inc(consts, 1)
            nc.gpsimd.memset(eps_col[:, :], LN_EPS).then_inc(consts, 1)
            pool.wait_ge(consts, 9)
            nc.gpsimd.memset(KTe[W4:P, :, :].bitcast(F32), 0.0).then_inc(consts, 1)
            pool.wait_ge(consts, 10)
            nc.gpsimd.memset(KTo[0:W4, :, :].bitcast(F32), 0.0).then_inc(consts, 1)
            pool.wait_ge(consts, 11)
            nc.gpsimd.memset(v_ones[:, :, :, HD:2 * HD], 1.0).then_inc(consts, 1)

            def stack_q_lo(tt):
                par = tt % 2
                pool.wait_ge(q_hi, tt + 1)
                q = qkv_rows[:, par, 0:D].rearrange("p (h d) -> p h d", d=HD)
                nc.gpsimd.tensor_tensor(q_stack[:, par, :, 2 * HD:EXTRA].bitcast(F32R), q,
                                        q_stack[:, par, :, 0:HD], ALU.subtract).then_inc(q_lo, 1)

            def mask(s):
                diag = probs[:, s % 2, 0:2].rearrange("p c h q -> p (c h q)")
                pool.wait_ge(exp_done, 3 * (s + 1))
                nc.gpsimd.affine_select(out=diag, in_=diag, compare_op=ALU.is_ge, fill=0.0, base=0,
                                        pattern=[[0, 2 * REP], [1, P]], channel_multiplier=-1).then_inc(causal, 1)

            for half in range(2):
                for tt in range(TTH * half, TTH * (half + 1)):
                    stack_q_lo(tt)
                for li in range(SH):
                    mask(SH * half + li)
                    if half == 1 and li % 2 == 0:
                        tt = li // 2
                        if li == 0:
                            pool.wait_ge(x1_in, 16)
                            pool.wait_ge(bias_in, 32)
                        nc.gpsimd.tensor_tensor(x1[:, tt, :], x1[:, tt, :], bo_rows[:, :], ALU.add).then_inc(x_bo, 1)

        @block.tensor
        def _(pe):
            def mm(out, lhsT, rhs, start, stop, shared=False):
                return nc.tensor.matmul(out, lhsT, rhs, start=start, stop=stop, skip_group_check=shared)

            def qkv(tt):
                tok = slice(tt % TTH * P, tt % TTH * P + P)
                for part, (cols, b, done, free) in enumerate((
                        (slice(0, D), bank[tt % 2], q_done, q_biased),
                        (slice(D, QKV), bank[2 + tt % 2], kv_done, kv_biased))):
                    if tt >= 2:
                        pe.wait_ge(free, tt - 1)
                    for c in range(C):
                        if part == 0:
                            if tt == 0:
                                pe.wait_ge(w_hi, c + 1)
                                pe.wait_ge(w_lo, c + 1)
                            if tt % TTH == 0:
                                pe.wait_ge(x_hi, C * (tt // TTH) + c + 1)
                                pe.wait_ge(x_lo, C * (tt // TTH) + c + 1)
                        o = b[:, 0:cols.stop - cols.start]
                        mm(o, xh[:, c, tok], wh[:, c, cols], c == 0, False)
                        mm(o, xh[:, c, tok], wl[:, c, cols], False, False)
                        last = mm(o, xl[:, c, tok], wh[:, c, cols], False, c == C - 1)
                    last.then_inc(done, 1)

            def transpose_stacks(tt):
                par = tt % 2
                for j in range(TR):
                    n = TR * tt + j
                    if tt % TTH or j >= 4:
                        pe.wait_ge(t_dve if j % 2 else t_act, (n - 4) // 2 + 1)
                    if j == 0:
                        pe.wait_ge(q_lo, tt + 1)
                    if j == TR - KV // 4:
                        pe.wait_ge(k_lo, tt + 1)
                    for k in range(4):
                        if j < H // 8:
                            src = q_stack[:, par, 2 * (4 * j + k):2 * (4 * j + k) + 2, :].rearrange("p h r -> p (h r)")
                        else:
                            src = k_stack[:, par, 4 * (j - H // 8) + k, :]
                        last = nc.tensor.transpose(bank[4 + n % 4][:, k * P:(k + 1) * P], src, identity[:, :])
                    last.then_inc(stack_t, 1)

            def scores0(s):
                b, g, bh = at(s)
                if s % SH:
                    pe.wait_ge(max0, s)
                mm(bank[0][:, :], identity_bf[:, :], later_keys[:, :, :].rearrange("p h k -> p (h k)"), True, False, True)
                for j in range(REP):
                    last = mm(bank[0][:, j * P:(j + 1) * P], QT[:, 2 * g + j // 2, bh * T:bh * T + P],
                              (KTe, KTo)[j % 2][:, g, bh * T:bh * T + P], False, j == REP - 1, True)
                last.then_inc(s0_done, 1)

            def scores1(s):
                b, g, bh = at(s)
                if s % SH:
                    pe.wait_ge(max1, s)
                for a in range(2):
                    o = bank[1 + a][:, :].rearrange("p (h k) -> p h k", h=2)
                    mm(o[:, :, P:T], identity_bf[:, :], later_keys[:, 0:2, :], True, False, True)
                    for j in (2 * a, 2 * a + 1):
                        last = mm(o[:, j % 2, :], QT[:, 2 * g + j // 2, bh * T + P:bh * T + T],
                                  (KTe, KTo)[j % 2][:, g, bh * T:bh * T + T], False, j % 2 == 1, True)
                last.then_inc(s1_done, 1)

            def transpose_maxima(u):
                pe.wait_ge(max1, UNIT * (u + 1))
                pe.wait_ge(max0, UNIT * (u + 1))
                if o_transposed[0]:
                    pe.wait_ge(o_norm, o_transposed[0])
                for qt in range(2):
                    last = nc.tensor.transpose(bank[7][0:UH, qt * P:(qt + 1) * P], neg_max[:, u % 2, qt, :], identity[:, :])
                last.then_inc(max_t, 1)

            def scores_t(s):
                b, g, bh = at(s)
                pe.wait_ge(max_in, 64 * (s // UNIT + 1))
                q = QT[:, 2 * g:2 * g + 2, bh * T:bh * T + T]
                for a, KT in enumerate((KTe, KTo)):
                    if s % SH:
                        pe.wait_ge(exp_done, 3 * (s - 1) + a + 1)
                    mm(bank[3 + a][:, :], KT[:, g, bh * T:bh * T + P], q, True, True).then_inc(st_done, 1)
                if s % SH:
                    pe.wait_ge(exp_done, 3 * s)
                for a, KT in enumerate((KTe, KTo)):
                    last = mm(bank[5][:, a * T:(a + 1) * T], KT[:, g, bh * T + P:bh * T + T], q[:, :, P:T], True, True, True)
                last.then_inc(st_done, 1)

            def pv(s):
                b, g, bh = at(s)
                pe.wait_ge(causal, s + 1)
                if s % SH:
                    pe.wait_ge(o_out, s)
                for j in range(REP):
                    mm(bank[6][32 * j:32 * j + 32, 0:T], v_ones[:, 2 * b, g, :], probs[:, s % 2, 0:3:2, j, :], True, False, True)
                for j in range(REP):
                    last = mm(bank[6][32 * j:32 * j + 32, P:T], v_ones[:, 2 * b + 1, g, :], probs[:, s % 2, 1, j, :],
                              False, True, True)
                last.then_inc(pv_done, 1)

            o_transposed, max_transposed = [0], [0]

            def transpose_o(s):
                pe.wait_ge(o_out, s + 1)
                pe.wait_ge(max_lo, max_transposed[0])
                if s:
                    pe.wait_ge(o_norm, s)
                for qt in range(2):
                    last = nc.tensor.transpose(bank[7][:, qt * P:(qt + 1) * P], o_cols[:, s % 2, qt * P:(qt + 1) * P],
                                               identity[:, :])
                last.then_inc(o_t, 1)
                o_transposed[0] = s + 1

            pe.wait_ge(consts, 12)
            for half in range(2):
                t0, s0 = TTH * half, SH * half
                for tt in range(t0, t0 + TTH + 1):
                    if half and tt == t0:
                        pe.wait_ge(max0, s0)
                        pe.wait_ge(max1, s0)
                    if tt < t0 + TTH:
                        qkv(tt)
                    if half and tt == t0:
                        pe.wait_ge(exp_done, 3 * s0)
                        pe.wait_ge(o_norm, s0)
                    if tt > t0:
                        transpose_stacks(tt - 1)
                pe.wait_ge(t_act, TR // 2 * (t0 + TTH))
                pe.wait_ge(t_dve, TR // 2 * (t0 + TTH))
                pe.wait_ge(v_in, t0 + TTH)
                for li in range(SH + LAGT):
                    s = s0 + li
                    if li < SH:
                        scores0(s)
                    if li and li % UNIT == 0 and li <= SH:
                        transpose_maxima(s // UNIT - 1)
                        max_transposed[0] = s // UNIT
                    if LAG2 <= li < SH + LAG2:
                        scores_t(s - LAG2)
                    if li < SH:
                        scores1(s)
                    if LAGV <= li < SH + LAGV:
                        pv(s - LAGV)
                    if li >= LAGT:
                        transpose_o(s - LAGT)

            def transpose_ot(tt):
                if tt >= 2:
                    pe.wait_ge(ot_lo, tt - 1)
                for c in range(C):
                    last = nc.tensor.transpose(bank[tt % 2][:, c * P:(c + 1) * P], o_tok[:, tt, c * P:(c + 1) * P],
                                               identity[:, :])
                last.then_inc(ot_done, 1)

            def project(tt):
                pe.wait_ge(ot_hi, tt + 1)
                pe.wait_ge(ot_lo, tt + 1)
                if tt >= 2:
                    pe.wait_ge(y_done, tt - 1)
                o = bank[2 + tt % 2][:, :]
                for c in range(C):
                    mm(o, oh[:, tt % 2, c, :], woh[:, c, :], c == 0, False)
                    mm(o, oh[:, tt % 2, c, :], wol[:, c, :], False, False)
                    last = mm(o, ol[:, tt % 2, c, :], woh[:, c, :], False, c == C - 1)
                last.then_inc(wo_done, 1)

            def transpose_x1(tt):
                pe.wait_ge(x1_done, tt + 1)
                if tt >= 2:
                    pe.wait_ge(x1_lo, tt - 1)
                for c in range(C):
                    last = nc.tensor.transpose(bank[4 + tt % 2][:, c * P:(c + 1) * P], x1[:, tt, c * P:(c + 1) * P],
                                               identity[:, :])
                last.then_inc(x1_t, 1)

            pe.wait_ge(o_norm, STEPS)
            pe.wait_ge(max0, STEPS)
            pe.wait_ge(max1, STEPS)
            pe.wait_ge(exp_done, 3 * STEPS)
            pe.wait_ge(wo_hi, C)
            pe.wait_ge(wo_lo, C)
            transpose_ot(0)
            for tt in range(TT + 2):
                if tt + 1 < TT:
                    transpose_ot(tt + 1)
                if tt < TT:
                    project(tt)
                if tt >= 2:
                    transpose_x1(tt - 2)

            def gate_up(k, unit):
                slot, tok = k // 2, slice(k % 2 * HALF, k % 2 * HALF + HALF)
                for m, (free, done) in enumerate(((silu_done, gate_done), (val_done, up_done))):
                    if unit is not None:
                        pe.wait_ge(free, unit - 3)
                    o = bank[2 * k + m][:, :]
                    for c in range(C):
                        mm(o, guh[:, slot, m, c, :], x1h[:, c, tok], c == 0, False)
                        mm(o, guh[:, slot, m, c, :], x1l[:, c, tok], False, False)
                        last = mm(o, gul[:, slot, m, c, :], x1h[:, c, tok], False, c == C - 1)
                    last.then_inc(done, 1)

            pe.wait_ge(x1_hi, TT)
            pe.wait_ge(x1_lo, TT)
            for k in range(4):
                if k % 2 == 0:
                    pe.wait_ge(gu_hi, k // 2 + 1)
                    pe.wait_ge(gu_lo, k // 2 + 1)
                gate_up(k, None)
            with pe.Fori(1, PAIRED) as i:
                for k in range(4):
                    if k % 2 == 0:
                        pe.wait_ge(gu_hi, 2 * i + (k // 2 + 1))
                        pe.wait_ge(gu_lo, 2 * i + (k // 2 + 1))
                    gate_up(k, 4 * i + k)
            pe.wait_ge(gu_hi, I_TILES)
            pe.wait_ge(gu_lo, I_TILES)
            for k in range(2):
                gate_up(k, 4 * PAIRED + k)

            pe.wait_ge(val_done, 2 * I_TILES)
            pe.wait_ge(silu_done, 2 * I_TILES)
            pe.wait_ge(wd_hi, I_TILES)
            pe.wait_ge(wd_lo, I_TILES)
            for tt in range(TT):
                pe.wait_ge(inter_cast, tt + 1)
                if tt >= 2:
                    pe.wait_ge(dval_done, tt - 1)
                for t in range(I_TILES):
                    mm(bank[tt % 2][:, :], inter_r[:, tt % 2, t, :], wdh[:, t, :], t == 0, False)
                    last = mm(bank[tt % 2][:, :], inter_r[:, tt % 2, t, :], wdl[:, t, :], False, t == I_TILES - 1)
                last.then_inc(down_done, 1)

        @block.scalar
        def _(act):
            def split_x(c, half):
                nc.scalar.copy(xh[:, c, :], x_raw[:, c, :]).then_inc(x_hi, 1)

            for c in range(C):
                act.wait_ge(w_in[c], 16)
                nc.scalar.copy(wh[:, c, :], w_raw[:, c, :]).then_inc(w_hi, 1)
                act.wait_ge(x_in[c], 16)
                split_x(c, 0)

            def stack_hi(tt):
                par = tt % 2
                if tt >= 2:
                    act.wait_ge(stack_t, TR * (tt - 1))
                else:
                    act.wait_ge(consts, 12)
                act.wait_ge(q_biased, tt + 1)
                q = qkv_rows[:, par, 0:D].rearrange("p (h d) -> p h d", d=HD)
                nc.scalar.copy(q_stack[:, par, :, 0:2 * HD].rearrange("p h (r d) -> p h r d", d=HD).bitcast(F32R),
                               q.unsqueeze(2).to_broadcast([P, H, 2, HD])).then_inc(q_hi, 1)
                act.wait_ge(kv_biased, tt + 1)
                k = qkv_rows[:, par, D:D + KVD].rearrange("p (h d) -> p h d", d=HD)
                nc.scalar.copy(k_stack[:, par].rearrange("p h (r d) -> p h r d", d=HD)[:, :, 0:8:2, :].bitcast(F32R),
                               k.unsqueeze(2).to_broadcast([P, KV, 4, HD])).then_inc(k_hi, 1)

            def copy_stacks(tt):
                tok = slice(tt % TTH * P, tt % TTH * P + P)
                for j in range(0, TR, 2):
                    n = TR * tt + j
                    act.wait_ge(stack_t, n + 1)
                    out_of_bank(nc.scalar.copy, n, j, tok, t_act)

            def step(li, half):
                s0 = SH * half
                s = s0 + li
                if LAG2 <= li < SH + LAG2:
                    e = s - LAG2
                    p = probs[:, e % 2]
                    for a in range(3):
                        act.wait_ge(st_done, 3 * e + a + 1)
                        if a == 0 and e >= 2:
                            act.wait_ge(pv_done, e - 1)
                        if a < 2:
                            dst = p[:, 0:3:2, a:REP:2, :].rearrange("p c h q -> p h c q")
                            src = bank[3 + a][:, :].rearrange("p (h c q) -> p h c q", h=2, c=2)
                        else:
                            dst = p[:, 1].rearrange("p (c a) q -> p a c q", a=2)
                            src = bank[5][:, :].rearrange("p (a c q) -> p a c q", a=2, c=2)
                        nc.scalar.activation(dst, src, ACT.Exp, scale=SCALE).then_inc(exp_done, 1)
                if LAGV <= li < SH + LAGV:
                    e = s - LAGV
                    act.wait_ge(pv_done, e + 1)
                    if e >= 2:
                        act.wait_ge(o_t, e - 1)
                    nc.scalar.copy(o_cols[:, e % 2, :], bank[6][:, 0:T]).then_inc(o_out, 1)

            for half in range(2):
                t0 = TTH * half
                for tt in range(t0, t0 + TTH + 1):
                    if tt < t0 + TTH:
                        stack_hi(tt)
                    if tt > t0:
                        copy_stacks(tt - 1)
                for li in range(SH + LAGT):
                    step(li, half)
                    if half == 0 and 1 <= li <= C:
                        if li == 1:
                            act.wait_ge(x2_in, 16)
                            act.wait_ge(kv_done, TTH)
                        split_x(li - 1, 1)
                    if half == 1 and 1 <= li <= C:
                        if li == 1:
                            act.wait_ge(wo_in, 16)
                        nc.scalar.copy(woh[:, li - 1, :], wo_raw[:, li - 1, :]).then_inc(wo_hi, 1)

            def deviation(var, n, done):
                act.wait_ge(var, n + 1)
                nc.scalar.activation(std[:, n % 2:n % 2 + 1], mean_var[:, n % 2, 1:2], ACT.Sqrt,
                                     bias=eps_col[:, 0:1]).then_inc(done, 1)

            act.wait_ge(o_norm, STEPS)
            act.wait_ge(causal, STEPS)
            def split_gate_up(slot, free=None):
                if free is not None:
                    act.wait_ge(up_done, free)
                nc.scalar.copy(guh[:, slot], gu_raw[:, slot]).then_inc(gu_hi, 1)

            for tt in range(TT + 2):
                if tt < TT:
                    act.wait_ge(ot_done, tt + 1)
                    if tt >= 2:
                        act.wait_ge(wo_done, tt - 1)
                    nc.scalar.copy(oh[:, tt % 2].rearrange("p c q -> p (c q)"), bank[tt % 2][:, :]).then_inc(ot_hi, 1)
                if 1 <= tt < TT + 1:
                    deviation(var_done, tt - 1, std_done)
                if tt >= 2:
                    act.wait_ge(x1_t, tt - 1)
                    nc.scalar.copy(x1h[:, :, (tt - 2) * P:(tt - 1) * P],
                                   bank[4 + tt % 2][:, :].rearrange("p (c q) -> p c q", c=C)).then_inc(x1_hi, 1)
                if tt == 2:
                    act.wait_ge(raw_in[0], 32)
                    split_gate_up(0)
                if tt == 3:
                    act.wait_ge(raw_in[1], 32)
                    split_gate_up(1)

            def split_down(t, slot):
                nc.scalar.copy(wdh[:, t, :], wd_raw[:, slot, :]).then_inc(wd_hi, 1)

            def silu_sign(k, unit):
                act.wait_ge(gate_done, unit + 1)
                if not (isinstance(unit, int) and unit < 2):
                    act.wait_ge(inter_done, unit - 1)
                nc.scalar.activation(silu_g[:, k % 2, :], bank[2 * k][:, :], ACT.Silu, scale=1.0 / 128).then_inc(silu_done, 1)
                act.wait_ge(val_done, unit + 1)
                nc.scalar.activation(sign[:, k % 2, :], val[:, k % 2, :], ACT.Sign).then_inc(sign_done, 1)

            act.wait_ge(wo_done, TT)
            for t in range(2):
                split_down(t, t)
            for k in range(4):
                silu_sign(k, k)
                if k % 2:
                    act.wait_ge(raw_in[k // 2], 64)
                    split_gate_up(k // 2, k + 1)
                    split_down(k // 2 + 2, k // 2)
            with act.Fori(1, PAIRED - 1) as i:
                for k in range(4):
                    silu_sign(k, 4 * i + k)
                    if k % 2:
                        act.wait_ge(raw_in[k // 2], 32 * i + 64)
                        split_gate_up(k // 2, 4 * i + (k + 1))
                        split_down(2 * i + (k // 2 + 2), k // 2)
            for k in range(4):
                silu_sign(k, 4 * (PAIRED - 1) + k)
                if k == 1:
                    act.wait_ge(raw_in[0], 32 * (PAIRED + 1))
                    split_gate_up(0, 4 * (PAIRED - 1) + 2)
                    split_down(I_TILES - 1, 0)
            for k in range(2):
                silu_sign(k, 4 * PAIRED + k)

            def cast(tt):
                if tt == 0:
                    act.wait_ge(inter_done, 2 * I_TILES)
                if tt >= 2:
                    act.wait_ge(down_done, tt - 1)
                nc.scalar.copy(inter_r[:, tt % 2], inter_q[:, :, tt * P:(tt + 1) * P]).then_inc(inter_cast, 1)

            cast(0)
            cast(1)
            for tt in range(TT):
                act.wait_ge(dval_done, tt + 1)
                if tt >= 2:
                    act.wait_ge(var2_done, tt - 1)
                nc.scalar.activation(sign[:, tt % 2, :], val[:, tt % 2, :], ACT.Sign).then_inc(dsign_done, 1)
                if tt + 2 < TT:
                    cast(tt + 2)
                deviation(var2_done, tt, std2_done)

        @block.vector
        def _(dve):
            steps = [0]

            def then(ins, base=0):
                ins.then_inc(dve_step, 1)
                steps[0] += 1
                dve.wait_ge(dve_step, base + steps[0])

            def split_x(c, half):
                dve.wait_ge(x_hi, C * half + c + 1)
                nc.vector.tensor_tensor(xl[:, c, :], x_raw[:, c, :], xh[:, c, :].bitcast(F32), ALU.subtract).then_inc(x_lo, 1)

            for c in range(C):
                dve.wait_ge(w_hi, c + 1)
                nc.vector.tensor_tensor(wl[:, c, :], w_raw[:, c, :], wh[:, c, :].bitcast(F32), ALU.subtract).then_inc(w_lo, 1)
                split_x(c, 0)
            dve.wait_ge(bias_in, 32)
            dve.wait_ge(consts, 12)

            def bias_qkv(tt):
                par = tt % 2
                if tt >= 2:
                    dve.wait_ge(q_lo, tt - 1)
                    dve.wait_ge(k_hi, tt - 1)
                dve.wait_ge(q_done, tt + 1)
                nc.vector.tensor_tensor(qkv_rows[:, par, 0:D], bank[tt % 2][:, :], bqkv_rows[:, 0:D], ALU.add).then_inc(q_biased, 1)
                dve.wait_ge(kv_done, tt + 1)
                nc.vector.tensor_tensor(qkv_rows[:, par, D:QKV], bank[2 + tt % 2][:, 0:2 * KVD], bqkv_rows[:, D:QKV],
                                        ALU.add).then_inc(kv_biased, 1)
                dve.wait_ge(kv_biased, tt + 1)
                nc.vector.tensor_copy(v_ones[:, tt, :, 0:HD], qkv_rows[:, par, D + KVD:QKV].rearrange("p (h d) -> p h d", d=HD)).then_inc(v_in, 1)
                k = qkv_rows[:, par, D:D + KVD].rearrange("p (h d) -> p h d", d=HD)
                blocks = k_stack[:, par].rearrange("p h (r d) -> p h r d", d=HD)
                dve.wait_ge(k_hi, tt + 1)
                nc.vector.tensor_tensor(blocks[:, :, 1:8:4, :].bitcast(F32R), k.unsqueeze(2).to_broadcast([P, KV, 2, HD]),
                                        blocks[:, :, 0:8:4, :], ALU.subtract).then_inc(k_lo, 1)

            def copy_stacks(tt):
                tok = slice(tt % TTH * P, tt % TTH * P + P)
                for j in range(1, TR, 2):
                    n = TR * tt + j
                    dve.wait_ge(stack_t, n + 1)
                    out_of_bank(nc.vector.tensor_copy, n, j, tok, t_dve)

            def step(li, half):
                s0 = SH * half
                s = s0 + li
                u, v = s // UNIT % 2, s % UNIT
                if li < SH:
                    if s // UNIT >= 2 and v == 0:
                        dve.wait_ge(max_t, s // UNIT - 1)
                    dve.wait_ge(s0_done, s + 1)
                    nc.vector.tensor_reduce(neg_max[:, u, 0, REP * v:REP * (v + 1)],
                                            bank[0][:, :].rearrange("p (h k) -> p h k", h=REP),
                                            AX.X, ALU.max, negate=True).then_inc(max0, 1)
                if li and li % UNIT == 0 and li <= SH:
                    m = s // UNIT - 1
                    dve.wait_ge(max_t, m + 1)
                    if m >= 2:
                        dve.wait_ge(max_in, 64 * (m - 1))
                    nc.vector.tensor_copy(max_rows[:, m % 2, 0, :], bank[7][0:UH, 0:T]).then_inc(max_hi, 1)
                    dve.wait_ge(max_hi, m + 1)
                    nc.vector.tensor_tensor(max_rows[:, m % 2, 1, :], bank[7][0:UH, 0:T],
                                            max_rows[:, m % 2, 0, :].bitcast(F32), ALU.subtract).then_inc(max_lo, 1)
                if li < SH:
                    dve.wait_ge(s1_done, s + 1)
                    for a in range(2):
                        ins = nc.vector.tensor_reduce(neg_max[:, u, 1, REP * v + 2 * a:REP * v + 2 * a + 2],
                                                      bank[1 + a][:, :].rearrange("p (h k) -> p h k", h=2),
                                                      AX.X, ALU.max, negate=True)
                    ins.then_inc(max1, 1)
                if li >= LAGT:
                    e = s - LAGT
                    b, g, _ = at(e)
                    o = bank[7][:, 0:2 * P].rearrange("p (t h r) -> p t h r", t=2, h=REP)
                    dve.wait_ge(o_t, e + 1)
                    nc.vector.reciprocal(inv_sum[:, :, :], o[:, :, :, HD]).then_inc(sum_inv, 1)
                    dve.wait_ge(sum_inv, e + 1)
                    nc.vector.tensor_tensor(
                        o_tok[:, 2 * b:2 * b + 2, g * REP * HD:(g + 1) * REP * HD].rearrange("p t (h d) -> p t h d", d=HD),
                        o[:, :, :, 0:HD], inv_sum[:, :, :].unsqueeze(3).to_broadcast([P, 2, REP, HD]),
                        ALU.mult).then_inc(o_norm, 1)

            for half in range(2):
                t0 = TTH * half
                for tt in range(t0, t0 + TTH + 1):
                    if tt < t0 + TTH:
                        bias_qkv(tt)
                    if tt > t0:
                        copy_stacks(tt - 1)
                for li in range(SH + LAGT):
                    step(li, half)
                    if half == 0 and 1 <= li <= C:
                        split_x(li - 1, 1)
                    if half == 1 and 1 <= li <= C:
                        dve.wait_ge(wo_hi, li)
                        nc.vector.tensor_tensor(wol[:, li - 1, :], wo_raw[:, li - 1, :], woh[:, li - 1, :].bitcast(F32),
                                                ALU.subtract).then_inc(wo_lo, 1)

            def moments(n, done):
                then(nc.vector.bn_stats(stats[:, :], y[:, n % 2, :]))
                nc.vector.bn_aggr(mean_var[:, n % 2, :], stats[:, :]).then_inc(done, 1)

            def normalise(dst, n, std_ready, done):
                dve.wait_ge(std_ready, n + 1)
                then(nc.vector.reciprocal(rstd[:, n % 2:n % 2 + 1], std[:, n % 2:n % 2 + 1]))
                nc.vector.tensor_scalar(dst, y[:, n % 2, :], mean_var[:, n % 2, 0:1], rstd[:, n % 2:n % 2 + 1],
                                        ALU.subtract, ALU.mult).then_inc(done, 1)

            def split_gate_up(slot, tile, free=None):
                dve.wait_ge(gu_hi, tile + 1)
                nc.vector.tensor_tensor(gul[:, slot], gu_raw[:, slot], guh[:, slot].bitcast(F32),
                                        ALU.subtract).then_inc(gu_lo, 1)

            dve.wait_ge(causal, STEPS)
            for tt in range(TT + 2):
                if tt < TT:
                    dve.wait_ge(ot_hi, tt + 1)
                    nc.vector.tensor_tensor(ol[:, tt % 2].rearrange("p c q -> p (c q)"), bank[tt % 2][:, :],
                                            oh[:, tt % 2].rearrange("p c q -> p (c q)").bitcast(F32),
                                            ALU.subtract).then_inc(ot_lo, 1)
                if 1 <= tt < TT + 1:
                    n = tt - 1
                    dve.wait_ge(wo_done, n + 1)
                    dve.wait_ge(x_bo, n + 1)
                    nc.vector.tensor_tensor(y[:, n % 2, :], bank[2 + n % 2][:, :], x1[:, n, :], ALU.add).then_inc(y_done, 1)
                    dve.wait_ge(y_done, n + 1)
                    moments(n, var_done)
                    normalise(x1[:, n, :], n, std_done, x1_done)
                if tt >= 2:
                    n = tt - 2
                    dve.wait_ge(x1_hi, n + 1)
                    tok = slice(n * P, (n + 1) * P)
                    nc.vector.tensor_tensor(x1l[:, :, tok], bank[4 + n % 2][:, :].rearrange("p (c q) -> p c q", c=C),
                                            x1h[:, :, tok].bitcast(F32), ALU.subtract).then_inc(x1_lo, 1)
                if tt in (2, 3):
                    split_gate_up(tt - 2, tt - 2)

            def split_down(t, slot):
                dve.wait_ge(wd_hi, t + 1)
                nc.vector.tensor_tensor(wdl[:, t, :], wd_raw[:, slot, :], wdh[:, t, :].bitcast(F32),
                                        ALU.subtract).then_inc(wd_lo, 1)

            def floor_magnitude(k, base):
                then(nc.vector.tensor_scalar(mag[:, k, :].bitcast(I32), val[:, k, :].bitcast(I32), ABS_12_BITS, None,
                                             ALU.bitwise_and), base)
                then(nc.vector.tensor_scalar(floor_mag[:, k, :], mag[:, k, :], TRUNC_OFFSET, 128.0, ALU.subtract, ALU.min), base)

            def quantise(k, t, unit, base=0):
                dve.wait_ge(up_done, unit + 1)
                dve.wait_ge(silu_done, unit + 1)
                nc.vector.tensor_tensor(val[:, k % 2, :], silu_g[:, k % 2, :], bank[2 * k + 1][:, :], ALU.mult).then_inc(val_done, 1)
                dve.wait_ge(val_done, unit + 1)
                floor_magnitude(k % 2, base)
                dve.wait_ge(sign_done, unit + 1)
                then(nc.vector.tensor_tensor(q_int[:, k % 2, :], floor_mag[:, k % 2, :], sign[:, k % 2, :], ALU.mult), base)
                nc.vector.tensor_scalar(inter_q[:, t, k % 2 * HALF:(k % 2 + 1) * HALF], q_int[:, k % 2, :], 127.0, None,
                                        ALU.min).then_inc(inter_done, 1)

            for t in range(2):
                split_down(t, t)
            for k in range(4):
                quantise(k, k // 2, k)
                if k % 2:
                    split_gate_up(k // 2, k // 2 + 2)
                    split_down(k // 2 + 2, k // 2)
            before = steps[0]
            PER_PAIR = 4 * 3
            with dve.Fori(1, PAIRED - 1) as i:
                for k in range(4):
                    quantise(k, 2 * i + k // 2, 4 * i + k, PER_PAIR * i - PER_PAIR)
                    if k % 2:
                        split_gate_up(k // 2, 2 * i + (k // 2 + 2))
                        split_down(2 * i + (k // 2 + 2), k // 2)
            assert steps[0] == before + PER_PAIR
            steps[0] = before + PER_PAIR * (PAIRED - 2)
            for k in range(4):
                quantise(k, 2 * (PAIRED - 1) + k // 2, 4 * (PAIRED - 1) + k)
                if k == 1:
                    split_gate_up(0, I_TILES - 1)
                    split_down(I_TILES - 1, 0)
            for k in range(2):
                quantise(k, I_TILES - 1, 4 * PAIRED + k)

            for tt in range(TT):
                k = tt % 2
                dve.wait_ge(down_done, tt + 1)
                nc.vector.tensor_scalar(val[:, k, :], bank[k][:, :], 128.0, None, ALU.mult).then_inc(dval_done, 1)
                dve.wait_ge(dval_done, tt + 1)
                floor_magnitude(k, 0)
                dve.wait_ge(dsign_done, tt + 1)
                then(nc.vector.tensor_tensor(q_int[:, k, :], floor_mag[:, k, :], sign[:, k, :], ALU.mult))
                if tt >= 2:
                    dve.wait_ge(stored[k], 16 * (tt // 2))
                then(nc.vector.scalar_tensor_tensor(out=y[:, k, :], in0=q_int[:, k, :], scalar=127.0, in1=x1[:, tt, :],
                                                    op0=ALU.min, op1=ALU.add))
                moments(tt, var2_done)
                normalise(y[:, k, :], tt, std2_done, out_done)


def kernel(L0_attn_x, L0_attn_Wq, L0_attn_bq, L0_attn_Wk, L0_attn_bk, L0_attn_Wv, L0_attn_bv, L0_attn_Wo, L0_attn_bo,
           L0_ffn_w_gate, L0_ffn_w_up, L0_ffn_w_down):
    import numpy as np
    import concourse.bacc as bacc
    from concourse.bass_utils import run_bass_kernel_spmd

    x = np.asarray(L0_attn_x)
    batches, tokens, width = x.shape
    x_tok = x.reshape(batches * tokens, width)
    gate, up, down = (np.asarray(w) for w in (L0_ffn_w_gate, L0_ffn_w_up, L0_ffn_w_down))
    inner = gate.shape[0]
    tiles = -(-inner // P)
    chunks = width // P

    def inner_tiles(w):
        padded = np.zeros((tiles * P, width), w.dtype)
        padded[:inner] = w
        return padded.reshape(tiles, P, chunks, P).transpose(0, 3, 2, 1)

    down_t = np.zeros((tiles * P, width), down.dtype)
    down_t[:inner] = down.T
    arrays = {
        "xT": x_tok.T,
        "x_tok": x_tok,
        "w_qkv": np.concatenate([np.asarray(w) for w in (L0_attn_Wq, L0_attn_Wk, L0_attn_Wv)], axis=1),
        "b_qkv": np.concatenate([np.asarray(b) for b in (L0_attn_bq, L0_attn_bk, L0_attn_bv)]),
        "w_o": np.asarray(L0_attn_Wo),
        "b_o": np.asarray(L0_attn_bo),
        "w_gate_up": np.stack([inner_tiles(gate), inner_tiles(up)], axis=2),
        "w_down": down_t.reshape(tiles, P, width),
    }
    arrays = {name: np.ascontiguousarray(a) for name, a in arrays.items()}
    nc = bacc.Bacc("TRN2", target_bir_lowering=False, num_devices=1)
    args = [nc.dram_tensor(name, a.shape, mybir.dt.from_np(a.dtype), kind="ExternalInput").ap() for name, a in arrays.items()]
    args.append(nc.dram_tensor("out", x_tok.shape, mybir.dt.from_np(x_tok.dtype), kind="ExternalOutput").ap())
    layer(nc, *args)
    got = run_bass_kernel_spmd(nc, [arrays], core_ids=[0]).results[0]["out"]
    return got.reshape(x.shape)
```

```python
from contextlib import ExitStack

import concourse.bass as bass
from concourse import mybir

ALU = mybir.AluOpType
ACT = mybir.ActivationFunctionType
AX = mybir.AxisListType
F32 = mybir.dt.float32
F32R = mybir.dt.float32r
BF16 = mybir.dt.bfloat16
I16 = mybir.dt.int16
I32 = mybir.dt.int32

P = 128
WARM_UP = 10
BANK = 512
LN_EPS = 1e-5
MASKED = -1e30
ROUND_TO_INT = 1.5 * 2.0 ** 23
TRUNC_OFFSET = 0.5 - 2.0 ** -13
ABS_12_BITS = 0x7FFFF000


def layer(nc, xT, x_tok, w_qkv, b_qkv, w_o, b_o, w_gate_up, w_down, out):
    D, N = xT.shape
    T = 256
    HD = 16
    H = D // HD
    KV = (w_qkv.shape[1] - D) // 2 // HD
    REP = H // KV
    NB = N // T
    TT = N // P
    C = D // P
    I_TILES = w_down.shape[0]
    HALF = N // 2
    TTH = TT // 2
    STEPS = NB * KV
    UNIT = 4
    UH = UNIT * REP
    KVD = KV * HD
    QKV = D + 2 * KVD
    W4 = 4 * HD
    EXTRA = 3 * HD
    LAG2, LAGV, LAGT = 6, 7, 8
    SCALE = float(HD) ** -0.5
    assert REP == 4 and C == 4 and T == 2 * P and QKV == 768

    ctx = ExitStack()
    with ctx:
        def keep(name, shape, dt):
            return ctx.enter_context(nc.sbuf_tensor(name, shape, dt))

        def sem(name):
            return ctx.enter_context(nc.semaphore(name))

        bank = [ctx.enter_context(nc.psum_tensor(f"bank{i}", [P, BANK], F32)) for i in range(8)]

        identity = keep("identity", [P, P], F32)
        identity_bf = keep("identity_bf", [P, P], BF16)
        later_keys = keep("later_keys", [P, REP, P], BF16)
        early_queries = keep("early_queries", [P, REP, P], BF16)
        bo_rows = keep("bo_rows", [P, D], F32)
        stats = keep("stats", [P, 6], F32)
        mean_var = keep("mean_var", [P, TT, 2], F32)
        std = keep("std", [P, TT], F32)
        rstd = keep("rstd", [P, TT], F32)
        eps_col = keep("eps_col", [P, 1], F32)

        def in_turn(stack):
            return lambda name, shape, dt: stack.enter_context(nc.sbuf_tensor(name, shape, dt))

        with ExitStack() as first:
            sb = in_turn(first)
            o_tok = sb("o_tok", [P, TT, D], F32)
            with ExitStack() as attention:
                sb = in_turn(attention)
                wh = sb("wqkv_hi", [P, C, QKV], F32R)
                wl = sb("wqkv_lo", [P, C, QKV], F32R)
                xh = sb("xT_hi", [P, C, HALF], F32R)
                xl = sb("xT_lo", [P, C, HALF], F32R)
                qkv_rows = sb("qkv_rows", [P, 2, QKV], F32)
                q_stack = sb("q_stack", [P, 2, H, W4], F32)
                k_stack = sb("k_stack", [P, 2, KV, W4], F32)
                bqkv_rows = sb("bqkv_rows", [P, QKV], F32)
                QT = sb("QT", [P, H // 2, HALF], F32R)
                KT = sb("KT", [P, 2, KV, HALF], F32R)
                v_ones = sb("v_ones", [P, TT, KV, 2 * HD], F32)
                probs = sb("probs", [P, 2, 3, REP, P], F32)
                neg_max = sb("neg_max", [P, 2, 2, UH], F32)
                max_rows = sb("max_rows", [UH, 2, 2, T], F32R)
                o_cols = sb("o_cols", [P, 2, T], F32)
                inv_sum = sb("inv_sum", [P, 2, REP], F32)
                w_raw = sb("wqkv_raw", [P, C, QKV], F32)
                x_raw = sb("xT_raw", [P, C, HALF], F32)
            with ExitStack() as projection:
                sb = in_turn(projection)
                wo_raw = sb("wo_raw", [P, C, D], F32)
                woh = sb("wo_hi", [P, C, D], F32R)
                wol = sb("wo_lo", [P, C, D], F32R)
        with ExitStack() as ffn:
            sb = in_turn(ffn)
            wdh = sb("w_down_hi", [P, I_TILES, D], F32R)
            wdl = sb("w_down_lo", [P, I_TILES, D], F32R)
            x1 = sb("x1", [P, TT, D], F32)
            oh = sb("oT_hi", [P, 2, C, P], F32R)
            ol = sb("oT_lo", [P, 2, C, P], F32R)
            gu_raw = sb("gate_up_raw", [P, 2, 2, C, P], F32)
            wd_raw = sb("w_down_raw", [P, 2, D], F32)
            y = sb("y", [P, 2, D], F32)
            x1h = sb("x1T_hi", [P, C, N], F32R)
            x1l = sb("x1T_lo", [P, C, N], F32R)
            inter_q = sb("inter_q", [P, I_TILES, N], F32R)
            silu_g = sb("silu_g", [P, 2, BANK], F32)
            val = sb("val", [P, 2, BANK], F32)
            mag = sb("mag", [P, 2, BANK], F32)
            floor_mag = sb("floor_mag", [P, 2, BANK], I16)
            sign = sb("sign", [P, 2, BANK], BF16)
            q_int = sb("q_int", [P, 2, BANK], BF16)
            guh = sb("gate_up_hi", [P, 2, 2, C, P], F32R)
            gul = sb("gate_up_lo", [P, 2, 2, C, P], F32R)

        w_in = [sem(f"w_in{c}") for c in range(C)]
        x_in = [sem(f"x_in{c}") for c in range(C)]
        x2_in, bias_in, max_in, wo_in, x1_in = sem("x2_in"), sem("bias_in"), sem("max_in"), sem("wo_in"), sem("x1_in")
        raw_in = [sem("raw_in0"), sem("raw_in1")]
        stored = [sem("stored0"), sem("stored1")]
        consts, zeroed = sem("consts"), sem("zeroed")
        w_hi, w_lo, x_hi, x_lo, x2_lo = sem("w_hi"), sem("w_lo"), sem("x_hi"), sem("x_lo"), sem("x2_lo")
        q_done, kv_done = sem("q_done"), sem("kv_done")
        q_biased, kv_biased = sem("q_biased"), sem("kv_biased")
        q_hi, k_hi, q_lo, k_lo, v_in = sem("q_hi"), sem("k_hi"), sem("q_lo"), sem("k_lo"), sem("v_in")
        stack_t = sem("stack_t")
        t_act, t_dve = sem("t_act"), sem("t_dve")
        s0_done, s1_done, max0, max1 = sem("s0_done"), sem("s1_done"), sem("max0"), sem("max1")
        max_t, max_hi, max_lo = sem("max_t"), sem("max_hi"), sem("max_lo")
        st_done, exp_done, pv_done = sem("st_done"), sem("exp_done"), sem("pv_done")
        o_out, o_t, sum_inv, o_norm = sem("o_out"), sem("o_t"), sem("sum_inv"), sem("o_norm")
        wo_hi, wo_lo, x_bo = sem("wo_hi_s"), sem("wo_lo_s"), sem("x_bo")
        ot_done, ot_hi, ot_lo, wo_done = sem("ot_done"), sem("ot_hi"), sem("ot_lo"), sem("wo_done")
        y_done, var_done, std_done, x1_done = sem("y_done"), sem("var_done"), sem("std_done"), sem("x1_done")
        x1_t, x1_hi, x1_lo = sem("x1_t"), sem("x1_hi"), sem("x1_lo")
        gu_hi, gu_lo, wd_hi, wd_lo = sem("gu_hi"), sem("gu_lo"), sem("wd_hi"), sem("wd_lo")
        gate_done, up_done, silu_done, val_done = sem("gate_done"), sem("up_done"), sem("silu_done"), sem("val_done")
        sign_done, inter_done = sem("sign_done"), sem("inter_done")
        down_done, dval_done, dsign_done = sem("down_done"), sem("dval_done"), sem("dsign_done")
        var2_done, std2_done, out_done = sem("var2_done"), sem("std2_done"), sem("out_done")
        dve_step = sem("dve_step")

        TR = H // 2 // 4 + 1
        T_ENG = TR // 2 + 1
        qkv_behind = {}
        stacks_behind = {0: 2, 1: 3}
        for b in range(2, NB):
            for k in range(2):
                qkv_behind[KV * b - 5 + k] = 2 * b + k
                stacks_behind[KV * b - 3 + k] = 2 * b + k
        assert LAG2 <= KV - 2
        X2_AT = range(4, 4 + C)
        WO_AT = range(26, 26 + C)
        GU_AT = range(30, 32)
        project_behind = {STEPS + k: k for k in range(TT - 2)}

        def at(s):
            return s // KV, s % KV, s // KV % (NB // 2)

        def ring(tt):
            return (5, 6, 7) if tt in (2, 3) else (1, 2, 0)

        def ot_bank(tt):
            return 7 if tt == TT - 1 else 0

        PAIRED = (I_TILES - 1) // 2

        def out_of_bank(copy, tt, j, done, half):
            tok = slice(tt % TTH * P, tt % TTH * P + P)
            src = bank[ring(tt)[j % 3]][:, :].rearrange("p (k q) -> p k q", k=4)
            if j < TR - 1:
                copy(QT[:, 4 * j:4 * j + 4, tok], src).then_inc(done, 1)
            else:
                keys = slice(W4 * half, W4 * half + W4)
                copy(KT[0:W4, 0, half:KV:2, tok], src[keys])
                copy(KT[W4:P, 1, half:KV:2, tok], src[keys]).then_inc(done, 1)

        block = ctx.enter_context(nc.Block())

        @block.sync
        def _(sp):
            for c in range(C):
                sp.dma_start(w_raw[:, c, :], w_qkv[c * P:(c + 1) * P, :]).then_inc(w_in[c], 16)
                sp.dma_start(x_raw[:, c, :], xT[c * P:(c + 1) * P, 0:HALF]).then_inc(x_in[c], 16)
            sp.dma_start(bqkv_rows[:, :], b_qkv.partition_broadcast(P)).then_inc(bias_in, 16)
            sp.dma_start(bo_rows[:, :], b_o.partition_broadcast(P)).then_inc(bias_in, 16)
            sp.wait_ge(x_lo, C)
            sp.wait_ge(x_hi, C)
            sp.dma_start(x_raw[:, :, :], xT[:, HALF:N].rearrange("(c p) n -> p c n", p=P)).then_inc(x2_in, 16)

            def maxima(u):
                b, g0 = u * UNIT // KV, u * UNIT % KV
                cols = slice(b % 2 * T, b % 2 * T + T)
                sp.wait_ge(max_lo, u + 1)
                sp.wait_ge(max_hi, u + 1)
                for j in range(2):
                    for r in range(2):
                        row = W4 * j + EXTRA + r
                        sp.dma_start(QT[row:row + 1, 2 * g0:2 * g0 + UH // 2, cols].bitcast(F32),
                                     max_rows[j:UH:2, u % 2, r, :].bitcast(F32)).then_inc(max_in, 16)

            for u in range(STEPS // UNIT - 2):
                maxima(u)
            sp.wait_ge(stack_t, TR * TT)
            sp.dma_start(wo_raw[:, :, :], w_o.rearrange("(c p) n -> p c n", p=P)).then_inc(wo_in, 16)
            sp.dma_start(x1[:, :, :], x_tok.rearrange("(t p) d -> p t d", p=P)).then_inc(x1_in, 16)

            def weights(t, slot):
                sp.dma_start(gu_raw[:, slot], w_gate_up[t]).then_inc(raw_in[slot], 16)
                sp.dma_start(wd_raw[:, slot], w_down[t]).then_inc(raw_in[slot], 16)

            weights(0, 0)
            weights(1, 1)
            for u in range(STEPS // UNIT - 2, STEPS // UNIT):
                maxima(u)
            with sp.Fori(1, PAIRED) as i:
                for k in range(2):
                    for split in (gu_hi, gu_lo, wd_hi, wd_lo):
                        sp.wait_ge(split, 2 * i + (k - 1))
                    weights(2 * i + k, k)
            for split in (gu_hi, gu_lo, wd_hi, wd_lo):
                sp.wait_ge(split, I_TILES - 2)
            weights(I_TILES - 1, 0)
            for tt in range(TT):
                sp.wait_ge(out_done, tt + 1)
                sp.dma_start(out[tt * P:(tt + 1) * P, :], y[:, tt % 2, :]).then_inc(stored[tt % 2], 16)
            for k in range(2):
                sp.wait_ge(stored[k], 16 * TT // 2)

        @block.gpsimd
        def _(pool):
            nc.gpsimd.memset(identity[:, :], 0.0).then_inc(zeroed, 1)
            nc.gpsimd.memset(identity_bf[:, :], 0.0).then_inc(zeroed, 1)
            nc.gpsimd.memset(later_keys[:, :, :], 0.0).then_inc(zeroed, 1)
            nc.gpsimd.memset(early_queries[:, :, :], 0.0).then_inc(zeroed, 1)
            pool.wait_ge(zeroed, 4)
            for m in (identity, identity_bf):
                nc.gpsimd.affine_select(out=m[:, :], in_=m[:, :], compare_op=ALU.not_equal, fill=1.0, base=0,
                                        pattern=[[-1, P]], channel_multiplier=1).then_inc(consts, 1)
            for m, sign_of_key in ((later_keys, -1), (early_queries, 1)):
                nc.gpsimd.affine_select(out=m[:, :, :], in_=m[:, :, :], compare_op=ALU.is_ge, fill=MASKED, base=0,
                                        pattern=[[0, REP], [sign_of_key, P]],
                                        channel_multiplier=-sign_of_key).then_inc(consts, 1)
            nc.gpsimd.memset(q_stack[:, :, :, EXTRA:W4], 0.0).then_inc(consts, 1)
            nc.gpsimd.memset(k_stack[:, :, :, EXTRA:EXTRA + 2], 1.0).then_inc(consts, 1)
            nc.gpsimd.memset(k_stack[:, :, :, EXTRA + 2:W4], 0.0).then_inc(consts, 1)
            nc.gpsimd.memset(eps_col[:, :], LN_EPS).then_inc(consts, 1)
            nc.gpsimd.memset(v_ones[:, :, :, HD:2 * HD], 1.0).then_inc(consts, 1)
            pool.wait_ge(consts, 9)
            nc.gpsimd.memset(KT[W4:P, 0, :, :].bitcast(F32), 0.0).then_inc(consts, 1)
            pool.wait_ge(consts, 10)
            nc.gpsimd.memset(KT[0:W4, 1, :, :].bitcast(F32), 0.0).then_inc(consts, 1)
            pool.wait_ge(consts, 11)

            def stack_lo(tt):
                par = tt % 2
                pool.wait_ge(q_hi, tt + 1)
                q = qkv_rows[:, par, 0:D].rearrange("p (h d) -> p h d", d=HD)
                nc.gpsimd.tensor_tensor(q_stack[:, par, :, 2 * HD:EXTRA].bitcast(F32R), q,
                                        q_stack[:, par, :, 0:HD], ALU.subtract).then_inc(q_lo, 1)
                pool.wait_ge(k_hi, tt + 1)
                k = qkv_rows[:, par, D:D + KVD].rearrange("p (h d) -> p h d", d=HD)
                nc.gpsimd.tensor_tensor(k_stack[:, par, :, HD:2 * HD].bitcast(F32R), k,
                                        k_stack[:, par, :, 0:HD], ALU.subtract).then_inc(k_lo, 1)

            for tt in range(TT):
                stack_lo(tt)
                if tt == TTH - 1:
                    for c in range(C):
                        pool.wait_ge(x_hi, C + c + 1)
                        nc.gpsimd.tensor_tensor(xl[:, c, :], x_raw[:, c, :], xh[:, c, :].bitcast(F32),
                                                ALU.subtract).then_inc(x2_lo, 1)
            for c in range(C):
                pool.wait_ge(wo_hi, c + 1)
                nc.gpsimd.tensor_tensor(wol[:, c, :], wo_raw[:, c, :], woh[:, c, :].bitcast(F32),
                                        ALU.subtract).then_inc(wo_lo, 1)
            pool.wait_ge(x1_in, 16)
            pool.wait_ge(bias_in, 32)
            for tt in range(TT):
                nc.gpsimd.tensor_tensor(x1[:, tt, :], x1[:, tt, :], bo_rows[:, :], ALU.add).then_inc(x_bo, 1)

            def gate_up_lo(t, slot):
                pool.wait_ge(gu_hi, t + 1)
                nc.gpsimd.tensor_tensor(gul[:, slot], gu_raw[:, slot], guh[:, slot].bitcast(F32),
                                        ALU.subtract).then_inc(gu_lo, 1)

            def down_lo(t, slot):
                pool.wait_ge(wd_hi, t + 1)
                nc.gpsimd.tensor_tensor(wdl[:, t, :], wd_raw[:, slot, :], wdh[:, t, :].bitcast(F32),
                                        ALU.subtract).then_inc(wd_lo, 1)

            for split_lo in (gate_up_lo, down_lo):
                for t in range(2):
                    split_lo(t, t)
            with pool.Fori(1, PAIRED) as i:
                for k in range(2):
                    gate_up_lo(2 * i + k, k)
                    down_lo(2 * i + k, k)
            gate_up_lo(I_TILES - 1, 0)
            down_lo(I_TILES - 1, 0)

        @block.tensor
        def _(pe):
            def mm(out, lhsT, rhs, start, stop, shared=False):
                return nc.tensor.matmul(out, lhsT, rhs, start=start, stop=stop, skip_group_check=shared)

            def qkv(tt, banks=(0, 1)):
                tok = slice(tt % TTH * P, tt % TTH * P + P)
                for part, (cols, done) in enumerate(((slice(0, D), q_done), (slice(D, QKV), kv_done))):
                    for c in range(C):
                        if part == 0:
                            if tt == 0:
                                pe.wait_ge(w_hi, c + 1)
                                pe.wait_ge(w_lo, c + 1)
                                pe.wait_ge(x_hi, c + 1)
                                pe.wait_ge(x_lo, c + 1)
                            if tt == TTH:
                                pe.wait_ge(x_hi, C + c + 1)
                                pe.wait_ge(x2_lo, c + 1)
                        o = bank[banks[part]][:, 0:cols.stop - cols.start]
                        mm(o, xh[:, c, tok], wh[:, c, cols], c == 0, False)
                        mm(o, xh[:, c, tok], wl[:, c, cols], False, False)
                        last = mm(o, xl[:, c, tok], wh[:, c, cols], False, c == C - 1)
                    last.then_inc(done, 1)

            def transpose_stacks(tt):
                par = tt % 2
                for j in range(TR):
                    if j == 0:
                        pe.wait_ge(q_lo, tt + 1)
                    if j == 3:
                        pe.wait_ge(t_act, T_ENG * tt + 1)
                    if j == TR - 1:
                        pe.wait_ge(t_dve, T_ENG * tt + 1)
                        pe.wait_ge(k_lo, tt + 1)
                    for k in range(4):
                        if j < TR - 1:
                            src = q_stack[:, par, 2 * (4 * j + k):2 * (4 * j + k) + 2, :].rearrange("p h r -> p (h r)")
                        else:
                            src = k_stack[:, par, 2 * k:2 * k + 2, :].rearrange("p h r -> p (h r)")
                        last = nc.tensor.transpose(bank[ring(tt)[j % 3]][:, k * P:(k + 1) * P], src, identity[:, :])
                    last.then_inc(stack_t, 1)

            def scores0(s):
                b, g, bh = at(s)
                if s:
                    pe.wait_ge(max0, s)
                if s - 1 in qkv_behind:
                    pe.wait_ge(q_biased, qkv_behind[s - 1] + 1)
                if stacks_behind.get(s - 1, 0) >= TTH:
                    pe.wait_ge(t_act, T_ENG * stacks_behind[s - 1] + 2)
                if g == 0:
                    pe.wait_ge(t_act, T_ENG * (2 * b + 2))
                    pe.wait_ge(t_dve, T_ENG * (2 * b + 2))
                    pe.wait_ge(v_in, 2 * b + 2)
                keys = slice(bh * T, bh * T + P)
                mm(bank[0][:, :], identity_bf[:, :], later_keys[:, :, :].rearrange("p h k -> p (h k)"), True, False, True)
                for c in range(2):
                    last = mm(bank[0][:, c * T:(c + 1) * T], QT[:, 2 * g + c, keys], KT[:, :, g, keys], False, c == 1, True)
                last.then_inc(s0_done, 1)

            def scores1(s):
                b, g, bh = at(s)
                if s:
                    pe.wait_ge(max1, s)
                if s - 1 in qkv_behind:
                    pe.wait_ge(kv_biased, qkv_behind[s - 1] + 1)
                if stacks_behind.get(s - 1, 0) >= TTH:
                    pe.wait_ge(t_act, T_ENG * (stacks_behind[s - 1] + 1))
                    pe.wait_ge(t_dve, T_ENG * (stacks_behind[s - 1] + 1))
                for c in range(2):
                    mm(bank[1 + c][:, :], QT[:, 2 * g + c, bh * T + P:bh * T + T], KT[:, :, g, bh * T:bh * T + T],
                       True, False, True)
                    last = mm(bank[1 + c][:, :].rearrange("p (h k) -> p h k", h=2)[:, :, P:T], identity_bf[:, :],
                              later_keys[:, 0:2, :], False, True, True)
                last.then_inc(s1_done, 1)

            def transpose_maxima(u):
                pe.wait_ge(max1, UNIT * (u + 1))
                pe.wait_ge(max0, UNIT * (u + 1))
                if o_transposed[0]:
                    pe.wait_ge(o_norm, o_transposed[0])
                elif u == 0:
                    pe.wait_ge(t_act, T_ENG * TTH)
                    pe.wait_ge(t_dve, T_ENG * TTH)
                for qt in range(2):
                    last = nc.tensor.transpose(bank[7][0:UH, qt * P:(qt + 1) * P], neg_max[:, u % 2, qt, :], identity[:, :])
                last.then_inc(max_t, 1)

            def scores_t(s):
                b, g, bh = at(s)
                pe.wait_ge(max_in, 64 * (s // UNIT + 1))
                q = QT[:, 2 * g:2 * g + 2, bh * T:bh * T + T]
                for a in range(2):
                    if s:
                        pe.wait_ge(exp_done, 3 * (s - 1) + a + 1)
                    elif a == 0:
                        pe.wait_ge(kv_biased, 4)
                    mm(bank[3 + a][:, :], KT[:, a, g, bh * T:bh * T + P], q, True, False, True)
                    mm(bank[3 + a][:, :].rearrange("p (h c q) -> p h c q", h=2, c=2)[:, :, 0, :], identity_bf[:, :],
                       early_queries[:, 0:2, :], False, True, True).then_inc(st_done, 1)
                if s:
                    pe.wait_ge(exp_done, 3 * s)
                mm(bank[5][:, :], identity_bf[:, :], early_queries[:, :, :].rearrange("p h q -> p (h q)"), True, False, True)
                for a in range(2):
                    last = mm(bank[5][:, a * T:(a + 1) * T], KT[:, a, g, bh * T + P:bh * T + T], q[:, :, P:T], False, a == 1, True)
                last.then_inc(st_done, 1)

            def pv(s):
                b, g, bh = at(s)
                pe.wait_ge(exp_done, 3 * (s + 1))
                if s:
                    pe.wait_ge(o_out, s)
                for j in range(REP):
                    mm(bank[6][32 * j:32 * j + 32, 0:T], v_ones[:, 2 * b, g, :], probs[:, s % 2, 0:3:2, j, :], True, False, True)
                for j in range(REP):
                    last = mm(bank[6][32 * j:32 * j + 32, P:T], v_ones[:, 2 * b + 1, g, :], probs[:, s % 2, 1, j, :],
                              False, True, True)
                last.then_inc(pv_done, 1)

            o_transposed, max_transposed = [0], [0]

            def transpose_o(s):
                pe.wait_ge(o_out, s + 1)
                pe.wait_ge(max_lo, max_transposed[0])
                if s:
                    pe.wait_ge(o_norm, s)
                for qt in range(2):
                    last = nc.tensor.transpose(bank[7][:, qt * P:(qt + 1) * P], o_cols[:, s % 2, qt * P:(qt + 1) * P],
                                               identity[:, :])
                last.then_inc(o_t, 1)
                o_transposed[0] = s + 1

            def transpose_ot(tt):
                if tt == TT - 1:
                    pe.wait_ge(ot_lo, tt - 1)
                elif tt:
                    pe.wait_ge(ot_lo, tt)
                else:
                    pe.wait_ge(max0, STEPS)
                    pe.wait_ge(max1, STEPS)
                    pe.wait_ge(wo_hi, C)
                    pe.wait_ge(wo_lo, C)
                pe.wait_ge(o_norm, KV * (tt // 2 + 1))
                for c in range(C):
                    last = nc.tensor.transpose(bank[ot_bank(tt)][:, c * P:(c + 1) * P], o_tok[:, tt, c * P:(c + 1) * P],
                                               identity[:, :])
                last.then_inc(ot_done, 1)

            def project(tt):
                pe.wait_ge(ot_hi, tt + 1)
                pe.wait_ge(ot_lo, tt + 1)
                if tt >= 2:
                    pe.wait_ge(y_done, tt - 1)
                o = bank[1 + tt % 2][:, :]
                for c in range(C):
                    mm(o, oh[:, tt % 2, c, :], woh[:, c, :], c == 0, False)
                    mm(o, oh[:, tt % 2, c, :], wol[:, c, :], False, False)
                    last = mm(o, ol[:, tt % 2, c, :], woh[:, c, :], False, c == C - 1)
                last.then_inc(wo_done, 1)

            def transpose_x1(tt):
                pe.wait_ge(x1_done, tt + 1)
                if tt == 0:
                    pe.wait_ge(exp_done, 3 * STEPS)
                    pe.wait_ge(o_out, STEPS)
                if tt >= 4:
                    pe.wait_ge(x1_lo, tt - 3)
                for c in range(C):
                    last = nc.tensor.transpose(bank[3 + tt % 4][:, c * P:(c + 1) * P], x1[:, tt, c * P:(c + 1) * P],
                                               identity[:, :])
                last.then_inc(x1_t, 1)

            pe.wait_ge(consts, 4)
            for _ in range(WARM_UP):
                mm(bank[7][:, :], identity_bf[:, :], later_keys[:, :, :].rearrange("p h k -> p (h k)"), True, True)
            qkv(0)
            qkv(1, (3, 4))
            qkv(2, (5, 6))
            pe.wait_ge(consts, 11)
            pe.wait_ge(q_biased, 1)
            pe.wait_ge(kv_biased, 1)
            transpose_stacks(0)
            pe.wait_ge(q_biased, 2)
            pe.wait_ge(kv_biased, 2)
            qkv(3, (3, 4))
            pe.wait_ge(t_act, T_ENG)
            pe.wait_ge(t_dve, T_ENG)
            transpose_stacks(1)
            for i in range(STEPS + LAGT):
                if i < STEPS:
                    scores0(i)
                if i and i % UNIT == 0 and i <= STEPS:
                    transpose_maxima(i // UNIT - 1)
                    max_transposed[0] = i // UNIT
                if i in project_behind:
                    transpose_ot(project_behind[i])
                if i < STEPS:
                    scores1(i)
                if LAG2 <= i < STEPS + LAG2:
                    scores_t(i - LAG2)
                if LAGV <= i < STEPS + LAGV:
                    pv(i - LAGV)
                if i >= LAGT:
                    transpose_o(i - LAGT)
                if i in qkv_behind:
                    pe.wait_ge(max0, i + 1)
                    pe.wait_ge(max1, i + 1)
                    qkv(qkv_behind[i])
                if i in stacks_behind:
                    tt = stacks_behind[i]
                    if tt >= TTH:
                        pe.wait_ge(max0, i + 1)
                        pe.wait_ge(max1, i + 1)
                    elif tt == 2:
                        pe.wait_ge(q_biased, 3)
                        pe.wait_ge(kv_biased, 3)
                    else:
                        pe.wait_ge(t_act, T_ENG * tt)
                        pe.wait_ge(t_dve, T_ENG * tt)
                    transpose_stacks(tt)
                if i in project_behind:
                    project(project_behind[i])
            transpose_x1(0)
            for tt in range(TT - 2, TT):
                transpose_ot(tt)
            transpose_x1(1)
            project(TT - 2)
            transpose_x1(2)
            project(TT - 1)
            transpose_x1(3)

            def gate_up(k, unit, between=None):
                slot, tok = k // 2, slice(k % 2 * HALF, k % 2 * HALF + HALF)
                for m, (free, done) in enumerate(((silu_done, gate_done), (val_done, up_done))):
                    if unit is not None:
                        pe.wait_ge(free, unit - 3)
                    o = bank[2 * k + m][:, :]
                    for c in range(C):
                        mm(o, guh[:, slot, m, c, :], x1h[:, c, tok], c == 0, False)
                        mm(o, guh[:, slot, m, c, :], x1l[:, c, tok], False, False)
                        last = mm(o, gul[:, slot, m, c, :], x1h[:, c, tok], False, c == C - 1)
                    last.then_inc(done, 1)
                    if between and m == 0:
                        between()

            def transpose_second_half():
                for tt in range(TTH, TT):
                    transpose_x1(tt)
                pe.wait_ge(y_done, TT - 1)

            for k in range(4):
                if k < 2:
                    pe.wait_ge(x1_hi, TTH * (k + 1))
                    pe.wait_ge(x1_lo, TTH * (k + 1))
                if k == 0:
                    pe.wait_ge(ot_lo, TT)
                if k == 1:
                    pe.wait_ge(y_done, TT)
                if k % 2 == 0:
                    pe.wait_ge(gu_hi, k // 2 + 1)
                    pe.wait_ge(gu_lo, k // 2 + 1)
                gate_up(k, None, transpose_second_half if k == 0 else None)
            with pe.Fori(1, PAIRED) as i:
                for k in range(4):
                    if k % 2 == 0:
                        pe.wait_ge(gu_hi, 2 * i + (k // 2 + 1))
                        pe.wait_ge(gu_lo, 2 * i + (k // 2 + 1))
                    gate_up(k, 4 * i + k)
            pe.wait_ge(gu_hi, I_TILES)
            pe.wait_ge(gu_lo, I_TILES)
            for k in range(2):
                gate_up(k, 4 * PAIRED + k)

            DOWN = (4, 5, 6, 7)
            pe.wait_ge(val_done, 2 * I_TILES - 2)
            pe.wait_ge(wd_hi, I_TILES)
            pe.wait_ge(wd_lo, I_TILES)
            for tt in range(TT):
                if tt >= 4:
                    pe.wait_ge(dval_done, tt - 3)
                tok = slice(tt * P, (tt + 1) * P)
                o = bank[DOWN[tt % 4]][:, :]
                for t in range(I_TILES):
                    if tt % TTH == 0 and t >= I_TILES - 2:
                        pe.wait_ge(inter_done, 2 * t + 1 + tt // TTH)
                    mm(o, inter_q[:, t, tok], wdh[:, t, :], t == 0, False)
                    last = mm(o, inter_q[:, t, tok], wdl[:, t, :], False, t == I_TILES - 1)
                last.then_inc(down_done, 1)

        @block.scalar
        def _(act):
            def split_x(c, half):
                nc.scalar.copy(xh[:, c, :], x_raw[:, c, :]).then_inc(x_hi, 1)

            for c in range(C):
                act.wait_ge(w_in[c], 16)
                nc.scalar.copy(wh[:, c, :], w_raw[:, c, :]).then_inc(w_hi, 1)
                act.wait_ge(x_in[c], 16)
                split_x(c, 0)

            def stack_hi(tt):
                par = tt % 2
                if tt >= 2:
                    act.wait_ge(stack_t, TR * (tt - 1))
                else:
                    act.wait_ge(consts, 11)
                act.wait_ge(q_biased, tt + 1)
                q = qkv_rows[:, par, 0:D].rearrange("p (h d) -> p h d", d=HD)
                nc.scalar.copy(q_stack[:, par, :, 0:2 * HD].rearrange("p h (r d) -> p h r d", d=HD).bitcast(F32R),
                               q.unsqueeze(2).to_broadcast([P, H, 2, HD])).then_inc(q_hi, 1)
                act.wait_ge(kv_biased, tt + 1)
                k = qkv_rows[:, par, D:D + KVD].rearrange("p (h d) -> p h d", d=HD)
                nc.scalar.copy(k_stack[:, par].rearrange("p h (r d) -> p h r d", d=HD)[:, :, 0:4:2, :].bitcast(F32R),
                               k.unsqueeze(2).to_broadcast([P, KV, 2, HD])).then_inc(k_hi, 1)

            def copy_stacks(tt):
                for j in (0, 2, TR - 1):
                    act.wait_ge(stack_t, TR * tt + j + 1)
                    out_of_bank(nc.scalar.copy, tt, j, t_act, 0)

            def o_hi(tt):
                act.wait_ge(ot_done, tt + 1)
                if tt >= 2:
                    act.wait_ge(wo_done, tt - 1)
                nc.scalar.copy(oh[:, tt % 2].rearrange("p c q -> p (c q)"), bank[ot_bank(tt)][:, :]).then_inc(ot_hi, 1)

            def probabilities(e):
                p = probs[:, e % 2]
                for a in range(3):
                    act.wait_ge(st_done, 3 * e + a + 1)
                    if a == 0 and e >= 2:
                        act.wait_ge(pv_done, e - 1)
                    if a < 2:
                        dst = p[:, 0:3:2, a:REP:2, :].rearrange("p c h q -> p h c q")
                        src = bank[3 + a][:, :].rearrange("p (h c q) -> p h c q", h=2, c=2)
                    else:
                        dst = p[:, 1].rearrange("p (c a) q -> p a c q", a=2)
                        src = bank[5][:, :].rearrange("p (a c q) -> p a c q", a=2, c=2)
                    nc.scalar.activation(dst, src, ACT.Exp, scale=SCALE).then_inc(exp_done, 1)

            def copy_o(e):
                act.wait_ge(pv_done, e + 1)
                if e >= 2:
                    act.wait_ge(o_t, e - 1)
                nc.scalar.copy(o_cols[:, e % 2, :], bank[6][:, 0:T]).then_inc(o_out, 1)

            def split_gate_up(slot, free=None):
                if free is not None:
                    act.wait_ge(up_done, free)
                nc.scalar.copy(guh[:, slot], gu_raw[:, slot]).then_inc(gu_hi, 1)

            def deviation(first, last, var, done):
                act.wait_ge(var, last)
                nc.scalar.activation(std[:, first:last], mean_var[:, first:last, 1], ACT.Sqrt,
                                     bias=eps_col[:, 0:1]).then_inc(done, 1)

            stack_hi(0)
            stack_hi(1)
            copy_stacks(0)
            stack_hi(2)
            copy_stacks(1)
            stack_hi(3)
            for i in range(STEPS + LAGT):
                if i in project_behind:
                    o_hi(project_behind[i])
                if LAG2 <= i < STEPS + LAG2:
                    probabilities(i - LAG2)
                if LAGV <= i < STEPS + LAGV:
                    copy_o(i - LAGV)
                if i in qkv_behind:
                    stack_hi(qkv_behind[i])
                if i in stacks_behind:
                    copy_stacks(stacks_behind[i])
                if i == STEPS + LAGV - 1:
                    deviation(0, TTH, var_done, std_done)
                if i in X2_AT:
                    if i == X2_AT[0]:
                        act.wait_ge(x2_in, 16)
                        act.wait_ge(kv_done, TTH)
                    split_x(i - X2_AT[0], 1)
                if i in WO_AT:
                    if i == WO_AT[0]:
                        act.wait_ge(wo_in, 16)
                    nc.scalar.copy(woh[:, i - WO_AT[0], :], wo_raw[:, i - WO_AT[0], :]).then_inc(wo_hi, 1)
                if i in GU_AT:
                    act.wait_ge(raw_in[i - GU_AT[0]], 32)
                    split_gate_up(i - GU_AT[0])


            def x1_high(tt):
                act.wait_ge(x1_t, tt + 1)
                nc.scalar.copy(x1h[:, :, tt * P:(tt + 1) * P],
                               bank[3 + tt % 4][:, :].rearrange("p (c q) -> p c q", c=C)).then_inc(x1_hi, 1)

            act.wait_ge(o_norm, STEPS)
            x1_high(0)
            for tt in range(TT - 2, TT):
                o_hi(tt)
            for tt in range(1, TTH):
                x1_high(tt)
            deviation(TTH, TT, var_done, std_done)
            for tt in range(TTH, TT):
                x1_high(tt)

            def split_down(t, slot):
                nc.scalar.copy(wdh[:, t, :], wd_raw[:, slot, :]).then_inc(wd_hi, 1)

            def silu_sign(k, unit):
                act.wait_ge(gate_done, unit + 1)
                if not (isinstance(unit, int) and unit < 2):
                    act.wait_ge(inter_done, unit - 1)
                nc.scalar.activation(silu_g[:, k % 2, :], bank[2 * k][:, :], ACT.Silu, scale=1.0 / 128).then_inc(silu_done, 1)
                act.wait_ge(val_done, unit + 1)
                nc.scalar.activation(sign[:, k % 2, :], val[:, k % 2, :], ACT.Sign).then_inc(sign_done, 1)

            act.wait_ge(wo_done, TT)
            for t in range(2):
                split_down(t, t)
            for k in range(4):
                silu_sign(k, k)
                if k % 2:
                    act.wait_ge(raw_in[k // 2], 64)
                    split_gate_up(k // 2, k + 1)
                    split_down(k // 2 + 2, k // 2)
            with act.Fori(1, PAIRED - 1) as i:
                for k in range(4):
                    silu_sign(k, 4 * i + k)
                    if k % 2:
                        act.wait_ge(raw_in[k // 2], 32 * i + 64)
                        split_gate_up(k // 2, 4 * i + (k + 1))
                        split_down(2 * i + (k // 2 + 2), k // 2)
            for k in range(4):
                silu_sign(k, 4 * (PAIRED - 1) + k)
                if k == 1:
                    act.wait_ge(raw_in[0], 32 * (PAIRED + 1))
                    split_gate_up(0, 4 * (PAIRED - 1) + 2)
                    split_down(I_TILES - 1, 0)
            for k in range(2):
                silu_sign(k, 4 * PAIRED + k)

            for tt in range(TT):
                act.wait_ge(dval_done, tt + 1)
                if tt >= 2:
                    act.wait_ge(var2_done, tt - 1)
                nc.scalar.activation(sign[:, tt % 2, :], val[:, tt % 2, :], ACT.Sign).then_inc(dsign_done, 1)
                deviation(tt, tt + 1, var2_done, std2_done)

        @block.vector
        def _(dve):
            steps = [0]

            def then(ins, base=0):
                ins.then_inc(dve_step, 1)
                steps[0] += 1
                dve.wait_ge(dve_step, base + steps[0])

            def split_x(c, half):
                dve.wait_ge(x_hi, C * half + c + 1)
                nc.vector.tensor_tensor(xl[:, c, :], x_raw[:, c, :], xh[:, c, :].bitcast(F32), ALU.subtract).then_inc(x_lo, 1)

            for c in range(C):
                dve.wait_ge(w_hi, c + 1)
                nc.vector.tensor_tensor(wl[:, c, :], w_raw[:, c, :], wh[:, c, :].bitcast(F32), ALU.subtract).then_inc(w_lo, 1)
                split_x(c, 0)
            dve.wait_ge(bias_in, 32)

            def bias_qkv(tt, banks=(0, 1)):
                par = tt % 2
                if tt >= 2:
                    dve.wait_ge(q_lo, tt - 1)
                    dve.wait_ge(k_lo, tt - 1)
                dve.wait_ge(q_done, tt + 1)
                nc.vector.tensor_tensor(qkv_rows[:, par, 0:D], bank[banks[0]][:, :], bqkv_rows[:, 0:D],
                                        ALU.add).then_inc(q_biased, 1)
                dve.wait_ge(kv_done, tt + 1)
                nc.vector.tensor_tensor(qkv_rows[:, par, D:QKV], bank[banks[1]][:, 0:2 * KVD], bqkv_rows[:, D:QKV],
                                        ALU.add).then_inc(kv_biased, 1)
                dve.wait_ge(kv_biased, tt + 1)
                nc.vector.tensor_copy(v_ones[:, tt, :, 0:HD],
                                      qkv_rows[:, par, D + KVD:QKV].rearrange("p (h d) -> p h d", d=HD)).then_inc(v_in, 1)

            def copy_stacks(tt):
                if tt == 0:
                    dve.wait_ge(consts, 11)
                for j in (1, 3, TR - 1):
                    dve.wait_ge(stack_t, TR * tt + j + 1)
                    out_of_bank(nc.vector.tensor_copy, tt, j, t_dve, 1)

            def maxima0(s):
                u, v = s // UNIT % 2, s % UNIT
                if s // UNIT >= 2 and v == 0:
                    dve.wait_ge(max_t, s // UNIT - 1)
                dve.wait_ge(s0_done, s + 1)
                nc.vector.tensor_reduce(neg_max[:, u, 0, REP * v:REP * (v + 1)],
                                        bank[0][:, :].rearrange("p (h k) -> p h k", h=REP),
                                        AX.X, ALU.max, negate=True).then_inc(max0, 1)

            def maxima1(s):
                u, v = s // UNIT % 2, s % UNIT
                dve.wait_ge(s1_done, s + 1)
                for a in range(2):
                    ins = nc.vector.tensor_reduce(neg_max[:, u, 1, REP * v + 2 * a:REP * v + 2 * a + 2],
                                                  bank[1 + a][:, :].rearrange("p (h k) -> p h k", h=2),
                                                  AX.X, ALU.max, negate=True)
                ins.then_inc(max1, 1)

            def split_maxima(m):
                dve.wait_ge(max_t, m + 1)
                if m >= 2:
                    dve.wait_ge(max_in, 64 * (m - 1))
                nc.vector.tensor_copy(max_rows[:, m % 2, 0, :], bank[7][0:UH, 0:T]).then_inc(max_hi, 1)
                dve.wait_ge(max_hi, m + 1)
                nc.vector.tensor_tensor(max_rows[:, m % 2, 1, :], bank[7][0:UH, 0:T],
                                        max_rows[:, m % 2, 0, :].bitcast(F32), ALU.subtract).then_inc(max_lo, 1)

            def normalise_o(e):
                b, g, _ = at(e)
                o = bank[7][:, 0:2 * P].rearrange("p (t h r) -> p t h r", t=2, h=REP)
                dve.wait_ge(o_t, e + 1)
                nc.vector.reciprocal(inv_sum[:, :, :], o[:, :, :, HD]).then_inc(sum_inv, 1)
                dve.wait_ge(sum_inv, e + 1)
                nc.vector.tensor_tensor(
                    o_tok[:, 2 * b:2 * b + 2, g * REP * HD:(g + 1) * REP * HD].rearrange("p t (h d) -> p t h d", d=HD),
                    o[:, :, :, 0:HD], inv_sum[:, :, :].unsqueeze(3).to_broadcast([P, 2, REP, HD]),
                    ALU.mult).then_inc(o_norm, 1)

            def o_lo(tt):
                dve.wait_ge(ot_hi, tt + 1)
                nc.vector.tensor_tensor(ol[:, tt % 2].rearrange("p c q -> p (c q)"), bank[ot_bank(tt)][:, :],
                                        oh[:, tt % 2].rearrange("p c q -> p (c q)").bitcast(F32),
                                        ALU.subtract).then_inc(ot_lo, 1)

            def add_residual(tt):
                dve.wait_ge(wo_done, tt + 1)
                dve.wait_ge(x_bo, tt + 1)
                nc.vector.tensor_tensor(x1[:, tt, :], bank[1 + tt % 2][:, :], x1[:, tt, :], ALU.add).then_inc(y_done, 1)
                dve.wait_ge(y_done, tt + 1)
                moments(x1[:, tt, :], tt, var_done)

            def moments(y, n, done):
                then(nc.vector.bn_stats(stats[:, :], y))
                nc.vector.bn_aggr(mean_var[:, n, :], stats[:, :]).then_inc(done, 1)

            def normalise(dst, y, n, done):
                nc.vector.tensor_scalar(dst, y, mean_var[:, n, 0:1], rstd[:, n:n + 1],
                                        ALU.subtract, ALU.mult).then_inc(done, 1)

            def low_x1(n):
                tok = slice(n * P, (n + 1) * P)
                dve.wait_ge(x1_hi, n + 1)
                nc.vector.tensor_tensor(x1l[:, :, tok], bank[3 + n % 4][:, :].rearrange("p (c q) -> p c q", c=C),
                                        x1h[:, :, tok].bitcast(F32), ALU.subtract).then_inc(x1_lo, 1)

            bias_qkv(0)
            bias_qkv(1, (3, 4))
            copy_stacks(0)
            bias_qkv(2, (5, 6))
            copy_stacks(1)
            bias_qkv(3, (3, 4))
            for i in range(STEPS + LAGT):
                if i < STEPS:
                    maxima0(i)
                if i and i % UNIT == 0 and i <= STEPS:
                    split_maxima(i // UNIT - 1)
                if i in project_behind:
                    o_lo(project_behind[i])
                if i < STEPS:
                    maxima1(i)
                if i == STEPS + LAGT - 1:
                    dve.wait_ge(std_done, 1)
                    then(nc.vector.reciprocal(rstd[:, 0:TTH], std[:, 0:TTH]))
                    normalise(x1[:, 0, :], x1[:, 0, :], 0, x1_done)
                if i >= LAGT:
                    normalise_o(i - LAGT)
                if i in qkv_behind:
                    bias_qkv(qkv_behind[i])
                if i in stacks_behind:
                    copy_stacks(stacks_behind[i])
                if i - 1 in project_behind:
                    add_residual(project_behind[i - 1])
            normalise(x1[:, 1, :], x1[:, 1, :], 1, x1_done)
            o_lo(TT - 2)
            o_lo(TT - 1)
            low_x1(0)
            normalise(x1[:, 2, :], x1[:, 2, :], 2, x1_done)
            low_x1(1)
            normalise(x1[:, 3, :], x1[:, 3, :], 3, x1_done)
            add_residual(TT - 2)
            low_x1(2)
            add_residual(TT - 1)
            low_x1(3)
            dve.wait_ge(std_done, 2)
            then(nc.vector.reciprocal(rstd[:, TTH:TT], std[:, TTH:TT]))
            for tt in range(TTH, TT):
                normalise(x1[:, tt, :], x1[:, tt, :], tt, x1_done)
                if tt > TTH:
                    low_x1(tt - 1)
            low_x1(TT - 1)

            def floor_magnitude(k, base):
                then(nc.vector.tensor_scalar(mag[:, k, :].bitcast(I32), val[:, k, :].bitcast(I32), ABS_12_BITS, None,
                                             ALU.bitwise_and), base)
                then(nc.vector.tensor_scalar(floor_mag[:, k, :], mag[:, k, :], TRUNC_OFFSET, 128.0, ALU.subtract, ALU.min), base)

            def quantise(k, t, unit, base=0):
                dve.wait_ge(up_done, unit + 1)
                dve.wait_ge(silu_done, unit + 1)
                nc.vector.tensor_tensor(val[:, k % 2, :], silu_g[:, k % 2, :], bank[2 * k + 1][:, :], ALU.mult).then_inc(val_done, 1)
                dve.wait_ge(val_done, unit + 1)
                floor_magnitude(k % 2, base)
                dve.wait_ge(sign_done, unit + 1)
                then(nc.vector.tensor_tensor(q_int[:, k % 2, :], floor_mag[:, k % 2, :], sign[:, k % 2, :], ALU.mult), base)
                nc.vector.tensor_scalar(inter_q[:, t, k % 2 * HALF:(k % 2 + 1) * HALF], q_int[:, k % 2, :], 127.0, None,
                                        ALU.min).then_inc(inter_done, 1)

            for k in range(4):
                quantise(k, k // 2, k)
            before = steps[0]
            PER_PAIR = 4 * 3
            with dve.Fori(1, PAIRED - 1) as i:
                for k in range(4):
                    quantise(k, 2 * i + k // 2, 4 * i + k, PER_PAIR * i - PER_PAIR)
            assert steps[0] == before + PER_PAIR
            steps[0] = before + PER_PAIR * (PAIRED - 2)
            for k in range(4):
                quantise(k, 2 * (PAIRED - 1) + k // 2, 4 * (PAIRED - 1) + k)
            for k in range(2):
                quantise(k, I_TILES - 1, 4 * PAIRED + k)

            for tt in range(TT):
                k = tt % 2
                dve.wait_ge(down_done, tt + 1)
                nc.vector.tensor_scalar(val[:, k, :], bank[4 + tt % 4][:, :], 128.0, None, ALU.mult).then_inc(dval_done, 1)
                dve.wait_ge(dval_done, tt + 1)
                floor_magnitude(k, 0)
                dve.wait_ge(dsign_done, tt + 1)
                then(nc.vector.tensor_tensor(q_int[:, k, :], floor_mag[:, k, :], sign[:, k, :], ALU.mult))
                if tt >= 2:
                    dve.wait_ge(stored[k], 16 * (tt // 2))
                then(nc.vector.scalar_tensor_tensor(out=y[:, k, :], in0=q_int[:, k, :], scalar=127.0, in1=x1[:, tt, :],
                                                    op0=ALU.min, op1=ALU.add))
                moments(y[:, k, :], tt, var2_done)
                dve.wait_ge(std2_done, tt + 1)
                then(nc.vector.reciprocal(rstd[:, tt:tt + 1], std[:, tt:tt + 1]))
                normalise(y[:, k, :], y[:, k, :], tt, out_done)


def kernel(L0_attn_x, L0_attn_Wq, L0_attn_bq, L0_attn_Wk, L0_attn_bk, L0_attn_Wv, L0_attn_bv, L0_attn_Wo, L0_attn_bo,
           L0_ffn_w_gate, L0_ffn_w_up, L0_ffn_w_down):
    import numpy as np
    import concourse.bacc as bacc
    from concourse.bass_utils import run_bass_kernel_spmd

    x = np.asarray(L0_attn_x)
    batches, tokens, width = x.shape
    x_tok = x.reshape(batches * tokens, width)
    gate, up, down = (np.asarray(w) for w in (L0_ffn_w_gate, L0_ffn_w_up, L0_ffn_w_down))
    inner = gate.shape[0]
    tiles = -(-inner // P)
    chunks = width // P

    def inner_tiles(w):
        padded = np.zeros((tiles * P, width), w.dtype)
        padded[:inner] = w
        return padded.reshape(tiles, P, chunks, P).transpose(0, 3, 2, 1)

    down_t = np.zeros((tiles * P, width), down.dtype)
    down_t[:inner] = down.T
    arrays = {
        "xT": x_tok.T,
        "x_tok": x_tok,
        "w_qkv": np.concatenate([np.asarray(w) for w in (L0_attn_Wq, L0_attn_Wk, L0_attn_Wv)], axis=1),
        "b_qkv": np.concatenate([np.asarray(b) for b in (L0_attn_bq, L0_attn_bk, L0_attn_bv)]),
        "w_o": np.asarray(L0_attn_Wo),
        "b_o": np.asarray(L0_attn_bo),
        "w_gate_up": np.stack([inner_tiles(gate), inner_tiles(up)], axis=2),
        "w_down": down_t.reshape(tiles, P, width),
    }
    arrays = {name: np.ascontiguousarray(a) for name, a in arrays.items()}
    nc = bacc.Bacc("TRN2", target_bir_lowering=False, num_devices=1)
    args = [nc.dram_tensor(name, a.shape, mybir.dt.from_np(a.dtype), kind="ExternalInput").ap() for name, a in arrays.items()]
    args.append(nc.dram_tensor("out", x_tok.shape, mybir.dt.from_np(x_tok.dtype), kind="ExternalOutput").ap())
    layer(nc, *args)
    got = run_bass_kernel_spmd(nc, [arrays], core_ids=[0]).results[0]["out"]
    return got.reshape(x.shape)
```

```python
from contextlib import ExitStack

import concourse.bass as bass
from concourse import mybir

ALU = mybir.AluOpType
ACT = mybir.ActivationFunctionType
AX = mybir.AxisListType
F32 = mybir.dt.float32
F32R = mybir.dt.float32r
BF16 = mybir.dt.bfloat16
I16 = mybir.dt.int16
I32 = mybir.dt.int32

P = 128
WARM_UP = 10
BANK = 512
LN_EPS = 1e-5
MASKED = -1e30
ROUND_TO_INT = 1.5 * 2.0 ** 23
TRUNC_OFFSET = 0.5 - 2.0 ** -13
ABS_12_BITS = 0x7FFFF000


def layer(nc, xT, x_tok, w_qkv, b_qkv, w_o, b_o, w_gate_up, w_down, out):
    D, N = xT.shape
    T = 256
    HD = 16
    H = D // HD
    KV = (w_qkv.shape[1] - D) // 2 // HD
    REP = H // KV
    NB = N // T
    TT = N // P
    C = D // P
    I_TILES = w_down.shape[0]
    HALF = N // 2
    TTH = TT // 2
    STEPS = NB * KV
    UNIT = 4
    UH = UNIT * REP
    KVD = KV * HD
    QKV = D + 2 * KVD
    W4 = 4 * HD
    EXTRA = 3 * HD
    LAG2, LAGV, LAGT = 6, 7, 8
    SCALE = float(HD) ** -0.5
    assert REP == 4 and C == 4 and T == 2 * P and QKV == 768

    ctx = ExitStack()
    with ctx:
        def keep(name, shape, dt):
            return ctx.enter_context(nc.sbuf_tensor(name, shape, dt))

        def sem(name):
            return ctx.enter_context(nc.semaphore(name))

        bank = [ctx.enter_context(nc.psum_tensor(f"bank{i}", [P, BANK], F32)) for i in range(8)]

        identity = keep("identity", [P, P], F32)
        identity_bf = keep("identity_bf", [P, P], BF16)
        later_keys = keep("later_keys", [P, REP, P], BF16)
        early_queries = keep("early_queries", [P, REP, P], BF16)
        bo_rows = keep("bo_rows", [P, D], F32)
        stats = keep("stats", [P, 2, 6], F32)
        mean_var = keep("mean_var", [P, TT, 2], F32)
        std = keep("std", [P, TT], F32)
        rstd = keep("rstd", [P, TT], F32)
        shift = keep("shift", [P, TT], F32)
        eps_col = keep("eps_col", [P, 1], F32)
        zeros = keep("zeros", [P, BANK], BF16)

        def in_turn(stack):
            return lambda name, shape, dt: stack.enter_context(nc.sbuf_tensor(name, shape, dt))

        with ExitStack() as first:
            sb = in_turn(first)
            o_tok = sb("o_tok", [P, TT, D], F32)
            with ExitStack() as attention:
                sb = in_turn(attention)
                wh = sb("wqkv_hi", [P, C, QKV], F32R)
                wl = sb("wqkv_lo", [P, C, QKV], F32R)
                xh = sb("xT_hi", [P, C, HALF], F32R)
                xl = sb("xT_lo", [P, C, HALF], F32R)
                qkv_rows = sb("qkv_rows", [P, 2, QKV], F32)
                q_stack = sb("q_stack", [P, 2, H, W4], F32)
                k_stack = sb("k_stack", [P, 2, KV, W4], F32)
                bqkv_rows = sb("bqkv_rows", [P, QKV], F32)
                QT = sb("QT", [P, H // 2, HALF], F32R)
                KT = sb("KT", [P, 2, KV, HALF], F32R)
                v_ones = sb("v_ones", [P, TT, KV, 2 * HD], F32)
                probs = sb("probs", [P, 2, 3, REP, P], F32)
                neg_max = sb("neg_max", [P, 2, 2, UH], F32)
                max_rows = sb("max_rows", [UH, 2, 2, T], F32R)
                o_cols = sb("o_cols", [P, 2, T], F32)
                inv_sum = sb("inv_sum", [P, 2, REP], F32)
                w_raw = sb("wqkv_raw", [P, C, QKV], F32)
                x_raw = sb("xT_raw", [P, C, HALF], F32)
            with ExitStack() as projection:
                sb = in_turn(projection)
                wo_raw = sb("wo_raw", [P, C, D], F32)
                woh = sb("wo_hi", [P, C, D], F32R)
                wol = sb("wo_lo", [P, C, D], F32R)
        with ExitStack() as ffn:
            sb = in_turn(ffn)
            wdh = sb("w_down_hi", [P, I_TILES, D], F32R)
            wdl = sb("w_down_lo", [P, I_TILES, D], F32R)
            x1 = sb("x1", [P, TT, D], F32)
            oh = sb("oT_hi", [P, 2, C, P], F32R)
            ol = sb("oT_lo", [P, 2, C, P], F32R)
            gu_raw = sb("gate_up_raw", [P, 2, 2, C, P], F32)
            wd_raw = sb("w_down_raw", [P, 2, D], F32)
            y = sb("y", [P, 2, D], F32)
            x1h = sb("x1T_hi", [P, C, N], F32R)
            x1l = sb("x1T_lo", [P, C, N], F32R)
            inter_q = sb("inter_q", [P, I_TILES, N], F32R)
            silu_g = sb("silu_g", [P, 2, BANK], F32)
            val = sb("val", [P, 2, BANK], F32)
            mag = sb("mag", [P, 2, BANK], F32)
            floor_mag = sb("floor_mag", [P, 2, BANK], I16)
            sign = sb("sign", [P, 2, BANK], BF16)
            q_int = sb("q_int", [P, 2, BANK], BF16)
            guh = sb("gate_up_hi", [P, 2, 2, C, P], F32R)
            gul = sb("gate_up_lo", [P, 2, 2, C, P], F32R)

        w_in = [sem(f"w_in{c}") for c in range(C)]
        x_in = [sem(f"x_in{c}") for c in range(C)]
        x_batch1_in, x2_in = sem("x_batch1_in"), sem("x2_in")
        bias_in, max_in, wo_in, x1_in = sem("bias_in"), sem("max_in"), sem("wo_in"), sem("x1_in")
        raw_in = [sem("raw_in0"), sem("raw_in1")]
        stored = [sem("stored0"), sem("stored1")]
        consts, zeroed, zeros_set = sem("consts"), sem("zeroed"), sem("zeros_set")
        w_hi, w_lo, x_hi, x_lo, x2_lo = sem("w_hi"), sem("w_lo"), sem("x_hi"), sem("x_lo"), sem("x2_lo")
        q_done, kv_done = sem("q_done"), sem("kv_done")
        q_biased, kv_biased = sem("q_biased"), sem("kv_biased")
        q_hi, k_hi, q_lo, k_lo, v_in = sem("q_hi"), sem("k_hi"), sem("q_lo"), sem("k_lo"), sem("v_in")
        stack_t = sem("stack_t")
        t_act, t_dve = sem("t_act"), sem("t_dve")
        s0_done, s1_done, max0, max1 = sem("s0_done"), sem("s1_done"), sem("max0"), sem("max1")
        max_t, max_hi, max_lo = sem("max_t"), sem("max_hi"), sem("max_lo")
        st_done, exp_done, pv_done = sem("st_done"), sem("exp_done"), sem("pv_done")
        o_out, o_t, sum_inv, o_norm = sem("o_out"), sem("o_t"), sem("sum_inv"), sem("o_norm")
        wo_hi, wo_lo, x_bo = sem("wo_is_hi"), sem("wo_is_lo"), sem("x_bo")
        ot_done, ot_hi, ot_lo, wo_done = sem("ot_done"), sem("ot_hi"), sem("ot_lo"), sem("wo_done")
        y_done, var_done, std_done, x1_done = sem("y_done"), sem("var_done"), sem("std_done"), sem("x1_done")
        x1_t, x1_hi, x1_lo = sem("x1_t"), sem("x1_hi"), sem("x1_lo")
        gu_hi, gu_lo, wd_hi, wd_lo = sem("gu_hi"), sem("gu_lo"), sem("wd_hi"), sem("wd_lo")
        gate_done, up_done, silu_done, val_done = sem("gate_done"), sem("up_done"), sem("silu_done"), sem("val_done")
        sign_done, inter_done = sem("sign_done"), sem("inter_done")
        down_done, dmag_done, dsign_done = sem("down_done"), sem("dmag_done"), sem("dsign_done")
        var2_done, std2_done, out_done = sem("var2_done"), sem("std2_done"), sem("out_done")
        shift_done, last_out_done = sem("shift_done"), sem("last_out_done")
        dve_step = sem("dve_step")

        TR = H // 2 // 4 + 1

        def copied_by(tt):
            if tt in (2, 3):
                return (0, 1, 2, 3, TR - 1), (TR - 1,)
            return ((0, 1, 3, TR - 1), (2, TR - 1)) if tt >= TTH else ((0, 2, TR - 1), (1, 3, TR - 1))

        def copies(engine, tt, j=TR - 1):
            return sum(len(copied_by(t)[engine]) for t in range(tt)) + copied_by(tt)[engine].index(j) + 1

        qkv_behind = {3: 4, 4: 5}
        stacks_behind = {0: 2, 2: 3}
        for b in range(2, NB):
            for k in range(2):
                if b > 2:
                    qkv_behind[KV * b - 7 + k] = 2 * b + k
                stacks_behind[KV * b - 3 + k] = 2 * b + k
        assert LAG2 <= KV - 2
        GU_AT = range(STEPS - 2, STEPS)
        WO_AT = range(STEPS - 2 - C, STEPS - 2)
        project_behind = {STEPS + 1 + k: k for k in range(TT - 2)}

        def at(s):
            return s // KV, s % KV, s // KV % (NB // 2)

        def qkv_banks(tt):
            return {1: (3, 4), 2: (5, 6), 3: (3, 4), 4: (3, 4), 5: (5, 6)}.get(tt, (0, 1))

        def ring(tt):
            return (5, 6, 7) if tt in (1, 2, 3) else (1, 2, 0)

        def ot_bank(tt):
            return 7 if tt == TT - 1 else 0

        def down_part(n):
            if n < TT - 1:
                return n, 0, slice(0, D), bank[4 + n % 4][:, :]
            half = n - (TT - 1)
            return TT - 1, half, slice(half * D // 2, (half + 1) * D // 2), bank[(7, 3)[half]][:, 0:D // 2]

        PAIRED = (I_TILES - 1) // 2

        def out_of_bank(copy, tt, j, done, half):
            tok = slice(tt % TTH * P, tt % TTH * P + P)
            src = bank[ring(tt)[j % 3]][:, :].rearrange("p (k q) -> p k q", k=4)
            if j < TR - 1:
                copy(QT[:, 4 * j:4 * j + 4, tok], src).then_inc(done, 1)
            else:
                keys = slice(W4 * half, W4 * half + W4)
                copy(KT[0:W4, 0, half:KV:2, tok], src[keys])
                copy(KT[W4:P, 1, half:KV:2, tok], src[keys]).then_inc(done, 1)

        block = ctx.enter_context(nc.Block())

        @block.sync
        def _(sp):
            for c in range(C):
                sp.dma_start(w_raw[:, c, :], w_qkv[c * P:(c + 1) * P, :]).then_inc(w_in[c], 16)
                sp.dma_start(x_raw[:, c, 0:T], xT[c * P:(c + 1) * P, 0:T]).then_inc(x_in[c], 16)
            sp.dma_start(x_raw[:, :, T:HALF], xT[:, T:HALF].rearrange("(c p) n -> p c n", p=P)).then_inc(x_batch1_in, 16)
            sp.dma_start(bqkv_rows[:, :], b_qkv.partition_broadcast(P)).then_inc(bias_in, 16)
            sp.dma_start(bo_rows[:, :], b_o.partition_broadcast(P)).then_inc(bias_in, 16)
            sp.wait_ge(x_lo, C + 1)
            sp.wait_ge(x_hi, C + 1)
            sp.dma_start(x_raw[:, :, :], xT[:, HALF:N].rearrange("(c p) n -> p c n", p=P)).then_inc(x2_in, 16)

            def maxima(u):
                b, g0 = u * UNIT // KV, u * UNIT % KV
                cols = slice(b % 2 * T, b % 2 * T + T)
                sp.wait_ge(max_lo, u + 1)
                sp.wait_ge(max_hi, u + 1)
                for j in range(2):
                    for r in range(2):
                        row = W4 * j + EXTRA + r
                        sp.dma_start(QT[row:row + 1, 2 * g0:2 * g0 + UH // 2, cols].bitcast(F32),
                                     max_rows[j:UH:2, u % 2, r, :].bitcast(F32)).then_inc(max_in, 16)

            for u in range(STEPS // UNIT - 2):
                maxima(u)
            sp.wait_ge(stack_t, TR * TT)

            def weights(t, slot):
                sp.dma_start(gu_raw[:, slot], w_gate_up[t]).then_inc(raw_in[slot], 16)
                sp.dma_start(wd_raw[:, slot], w_down[t]).then_inc(raw_in[slot], 16)

            weights(0, 0)
            weights(1, 1)
            for u in range(STEPS // UNIT - 2, STEPS // UNIT):
                maxima(u)
            with sp.Fori(1, PAIRED) as i:
                for k in range(2):
                    for split in (gu_hi, gu_lo, wd_hi, wd_lo):
                        sp.wait_ge(split, 2 * i + (k - 1))
                    weights(2 * i + k, k)
            for split in (gu_hi, gu_lo, wd_hi, wd_lo):
                sp.wait_ge(split, I_TILES - 2)
            weights(I_TILES - 1, 0)
            for tt in range(TT):
                if tt < TT - 1:
                    sp.wait_ge(out_done, tt + 1)
                else:
                    sp.wait_ge(last_out_done, 1)
                sp.dma_start(out[tt * P:(tt + 1) * P, :], y[:, tt % 2, :]).then_inc(stored[tt % 2], 16)
            for k in range(2):
                sp.wait_ge(stored[k], 16 * TT // 2)

        @block.gpsimd
        def _(pool):
            nc.gpsimd.memset(zeros[:, :], 0.0).then_inc(zeros_set, 1)
            nc.gpsimd.memset(identity[:, :], 0.0).then_inc(zeroed, 1)
            nc.gpsimd.memset(identity_bf[:, :], 0.0).then_inc(zeroed, 1)
            nc.gpsimd.memset(later_keys[:, :, :], 0.0).then_inc(zeroed, 1)
            nc.gpsimd.memset(early_queries[:, :, :], 0.0).then_inc(zeroed, 1)
            pool.wait_ge(zeroed, 4)
            for m in (identity, identity_bf):
                nc.gpsimd.affine_select(out=m[:, :], in_=m[:, :], compare_op=ALU.not_equal, fill=1.0, base=0,
                                        pattern=[[-1, P]], channel_multiplier=1).then_inc(consts, 1)
            for m, sign_of_key in ((later_keys, -1), (early_queries, 1)):
                nc.gpsimd.affine_select(out=m[:, :, :], in_=m[:, :, :], compare_op=ALU.is_ge, fill=MASKED, base=0,
                                        pattern=[[0, REP], [sign_of_key, P]],
                                        channel_multiplier=-sign_of_key).then_inc(consts, 1)
            nc.gpsimd.memset(q_stack[:, :, :, EXTRA:W4], 0.0).then_inc(consts, 1)
            nc.gpsimd.memset(k_stack[:, :, :, EXTRA:EXTRA + 2], 1.0).then_inc(consts, 1)
            nc.gpsimd.memset(k_stack[:, :, :, EXTRA + 2:W4], 0.0).then_inc(consts, 1)
            nc.gpsimd.memset(eps_col[:, :], LN_EPS).then_inc(consts, 1)
            nc.gpsimd.memset(v_ones[:, :, :, HD:2 * HD], 1.0).then_inc(consts, 1)
            pool.wait_ge(consts, 9)
            nc.gpsimd.memset(KT[W4:P, 0, :, :].bitcast(F32), 0.0).then_inc(consts, 1)
            pool.wait_ge(consts, 10)
            nc.gpsimd.memset(KT[0:W4, 1, :, :].bitcast(F32), 0.0).then_inc(consts, 1)
            pool.wait_ge(consts, 11)

            def stack_lo(tt):
                par = tt % 2
                pool.wait_ge(q_hi, tt + 1)
                q = qkv_rows[:, par, 0:D].rearrange("p (h d) -> p h d", d=HD)
                nc.gpsimd.tensor_tensor(q_stack[:, par, :, 2 * HD:EXTRA].bitcast(F32R), q,
                                        q_stack[:, par, :, 0:HD], ALU.subtract).then_inc(q_lo, 1)
                pool.wait_ge(k_hi, tt + 1)
                k = qkv_rows[:, par, D:D + KVD].rearrange("p (h d) -> p h d", d=HD)
                nc.gpsimd.tensor_tensor(k_stack[:, par, :, HD:2 * HD].bitcast(F32R), k,
                                        k_stack[:, par, :, 0:HD], ALU.subtract).then_inc(k_lo, 1)

            for tt in range(TT):
                stack_lo(tt)
                if tt == TTH - 1:
                    for c in range(C):
                        pool.wait_ge(x_hi, C + 1 + c + 1)
                        nc.gpsimd.tensor_tensor(xl[:, c, :], x_raw[:, c, :], xh[:, c, :].bitcast(F32),
                                                ALU.subtract).then_inc(x2_lo, 1)
            for c in range(C):
                pool.wait_ge(wo_hi, c + 1)
                nc.gpsimd.tensor_tensor(wol[:, c, :], wo_raw[:, c, :], woh[:, c, :].bitcast(F32),
                                        ALU.subtract).then_inc(wo_lo, 1)
            pool.wait_ge(x1_in, 16)
            pool.wait_ge(bias_in, 32)
            for tt in range(TT):
                nc.gpsimd.tensor_tensor(x1[:, tt, :], x1[:, tt, :], bo_rows[:, :], ALU.add).then_inc(x_bo, 1)

            def gate_up_lo(t, slot):
                pool.wait_ge(gu_hi, t + 1)
                nc.gpsimd.tensor_tensor(gul[:, slot], gu_raw[:, slot], guh[:, slot].bitcast(F32),
                                        ALU.subtract).then_inc(gu_lo, 1)

            def down_lo(t, slot):
                pool.wait_ge(wd_hi, t + 1)
                nc.gpsimd.tensor_tensor(wdl[:, t, :], wd_raw[:, slot, :], wdh[:, t, :].bitcast(F32),
                                        ALU.subtract).then_inc(wd_lo, 1)

            for split_lo in (gate_up_lo, down_lo):
                for t in range(2):
                    split_lo(t, t)
            with pool.Fori(1, PAIRED) as i:
                for k in range(2):
                    gate_up_lo(2 * i + k, k)
                    down_lo(2 * i + k, k)
            gate_up_lo(I_TILES - 1, 0)
            down_lo(I_TILES - 1, 0)

        @block.tensor
        def _(pe):
            def mm(out, lhsT, rhs, start, stop, shared=False):
                return nc.tensor.matmul(out, lhsT, rhs, start=start, stop=stop, skip_group_check=shared)

            def wait_copied(tt, j=TR - 1):
                if j in copied_by(tt)[0]:
                    pe.wait_ge(t_act, copies(0, tt, j))
                if j in copied_by(tt)[1]:
                    pe.wait_ge(t_dve, copies(1, tt, j))

            def qkv(*tiles):
                parts = ((slice(0, D), q_done), (slice(D, QKV), kv_done))
                for c in range(C):
                    if 0 in tiles:
                        pe.wait_ge(w_hi, c + 1)
                        pe.wait_ge(w_lo, c + 1)
                        pe.wait_ge(x_hi, c + 1)
                        pe.wait_ge(x_lo, c + 1)
                    if 2 in tiles and c == 0:
                        pe.wait_ge(x_hi, C + 1)
                        pe.wait_ge(x_lo, C + 1)
                    if TTH in tiles:
                        pe.wait_ge(x_hi, C + 1 + c + 1)
                        pe.wait_ge(x2_lo, c + 1)
                    for tt in tiles:
                        tok = slice(tt % TTH * P, tt % TTH * P + P)
                        for part, (cols, done) in enumerate(parts):
                            o = bank[qkv_banks(tt)[part]][:, 0:cols.stop - cols.start]
                            mm(o, xh[:, c, tok], wh[:, c, cols], c == 0, False)
                            mm(o, xh[:, c, tok], wl[:, c, cols], False, False)
                            last = mm(o, xl[:, c, tok], wh[:, c, cols], False, c == C - 1)
                            if c == C - 1:
                                last.then_inc(done, 1)

            def transpose_stacks(tt):
                par = tt % 2
                for j in range(TR):
                    if j == 0:
                        pe.wait_ge(q_lo, tt + 1)
                    if j >= 3:
                        wait_copied(tt, j - 3)
                    if j == TR - 1:
                        pe.wait_ge(k_lo, tt + 1)
                    for k in range(4):
                        if j < TR - 1:
                            src = q_stack[:, par, 2 * (4 * j + k):2 * (4 * j + k) + 2, :].rearrange("p h r -> p (h r)")
                        else:
                            src = k_stack[:, par, 2 * k:2 * k + 2, :].rearrange("p h r -> p (h r)")
                        last = nc.tensor.transpose(bank[ring(tt)[j % 3]][:, k * P:(k + 1) * P], src, identity[:, :])
                    last.then_inc(stack_t, 1)

            def scores0(s):
                b, g, bh = at(s)
                if s:
                    pe.wait_ge(max0, s)
                if qkv_behind.get(s - 1, 0) >= 6:
                    pe.wait_ge(q_biased, qkv_behind[s - 1] + 1)
                if stacks_behind.get(s - 1, 0) >= TTH:
                    wait_copied(stacks_behind[s - 1], 2)
                if g == 0:
                    wait_copied(2 * b + 1)
                    pe.wait_ge(v_in, 2 * b + 2)
                keys = slice(bh * T, bh * T + P)
                mm(bank[0][:, :], identity_bf[:, :], later_keys[:, :, :].rearrange("p h k -> p (h k)"), True, False, True)
                for c in range(2):
                    last = mm(bank[0][:, c * T:(c + 1) * T], QT[:, 2 * g + c, keys], KT[:, :, g, keys], False, c == 1, True)
                last.then_inc(s0_done, 1)

            def scores1(s):
                b, g, bh = at(s)
                if qkv_behind.get(s - 1, 0) >= 6:
                    pe.wait_ge(kv_biased, qkv_behind[s - 1] + 1)
                if stacks_behind.get(s - 1, 0) >= TTH:
                    wait_copied(stacks_behind[s - 1], 3)
                    wait_copied(stacks_behind[s - 1])
                for c in range(2):
                    if s:
                        pe.wait_ge(max1, 2 * s - 1 + c)
                    mm(bank[1 + c][:, :], QT[:, 2 * g + c, bh * T + P:bh * T + T], KT[:, :, g, bh * T:bh * T + T],
                       True, False, True)
                    mm(bank[1 + c][:, :].rearrange("p (h k) -> p h k", h=2)[:, :, P:T], identity_bf[:, :],
                       later_keys[:, 0:2, :], False, True, True).then_inc(s1_done, 1)

            def transpose_maxima(u):
                pe.wait_ge(max1, 2 * UNIT * (u + 1))
                pe.wait_ge(max0, UNIT * (u + 1))
                if o_transposed[0]:
                    pe.wait_ge(o_norm, o_transposed[0])
                elif u == 0:
                    wait_copied(TTH - 1)
                for qt in range(2):
                    last = nc.tensor.transpose(bank[7][0:UH, qt * P:(qt + 1) * P], neg_max[:, u % 2, qt, :], identity[:, :])
                last.then_inc(max_t, 1)

            def scores_t(s):
                b, g, bh = at(s)
                pe.wait_ge(max_in, 64 * (s // UNIT + 1))
                q = QT[:, 2 * g:2 * g + 2, bh * T:bh * T + T]
                for a in range(2):
                    if s:
                        pe.wait_ge(exp_done, 3 * (s - 1) + a + 1)
                    elif a == 0:
                        pe.wait_ge(kv_biased, 6)
                    mm(bank[3 + a][:, :], KT[:, a, g, bh * T:bh * T + P], q, True, False, True)
                    mm(bank[3 + a][:, :].rearrange("p (h c q) -> p h c q", h=2, c=2)[:, :, 0, :], identity_bf[:, :],
                       early_queries[:, 0:2, :], False, True, True).then_inc(st_done, 1)
                if s:
                    pe.wait_ge(exp_done, 3 * s)
                mm(bank[5][:, :], identity_bf[:, :], early_queries[:, :, :].rearrange("p h q -> p (h q)"), True, False, True)
                for a in range(2):
                    last = mm(bank[5][:, a * T:(a + 1) * T], KT[:, a, g, bh * T + P:bh * T + T], q[:, :, P:T], False, a == 1, True)
                last.then_inc(st_done, 1)

            def pv(s):
                b, g, bh = at(s)
                pe.wait_ge(exp_done, 3 * (s + 1))
                if s:
                    pe.wait_ge(o_out, s)
                for j in range(REP):
                    mm(bank[6][32 * j:32 * j + 32, 0:T], v_ones[:, 2 * b, g, :], probs[:, s % 2, 0:3:2, j, :], True, False, True)
                for j in range(REP):
                    last = mm(bank[6][32 * j:32 * j + 32, P:T], v_ones[:, 2 * b + 1, g, :], probs[:, s % 2, 1, j, :],
                              False, True, True)
                last.then_inc(pv_done, 1)

            o_transposed, max_transposed = [0], [0]

            def transpose_o(s):
                pe.wait_ge(o_out, s + 1)
                pe.wait_ge(max_lo, max_transposed[0])
                if s:
                    pe.wait_ge(o_norm, s)
                for qt in range(2):
                    last = nc.tensor.transpose(bank[7][:, qt * P:(qt + 1) * P], o_cols[:, s % 2, qt * P:(qt + 1) * P],
                                               identity[:, :])
                last.then_inc(o_t, 1)
                o_transposed[0] = s + 1

            def transpose_ot(tt):
                if tt == TT - 1:
                    pe.wait_ge(ot_lo, tt - 1)
                elif tt:
                    pe.wait_ge(ot_lo, tt)
                else:
                    pe.wait_ge(max0, STEPS)
                    pe.wait_ge(max1, 2 * STEPS)
                    pe.wait_ge(wo_hi, C)
                    pe.wait_ge(wo_lo, C)
                pe.wait_ge(o_norm, KV * (tt // 2 + 1))
                for c in range(C):
                    last = nc.tensor.transpose(bank[ot_bank(tt)][:, c * P:(c + 1) * P], o_tok[:, tt, c * P:(c + 1) * P],
                                               identity[:, :])
                last.then_inc(ot_done, 1)

            def project(tt):
                pe.wait_ge(ot_hi, tt + 1)
                pe.wait_ge(ot_lo, tt + 1)
                if tt >= 2:
                    pe.wait_ge(y_done, tt - 1)
                o = bank[1 + tt % 2][:, :]
                for c in range(C):
                    mm(o, oh[:, tt % 2, c, :], woh[:, c, :], c == 0, False)
                    mm(o, oh[:, tt % 2, c, :], wol[:, c, :], False, False)
                    last = mm(o, ol[:, tt % 2, c, :], woh[:, c, :], False, c == C - 1)
                last.then_inc(wo_done, 1)

            def transpose_x1(tt):
                pe.wait_ge(x1_done, tt + 1)
                if tt == 0:
                    pe.wait_ge(exp_done, 3 * STEPS)
                    pe.wait_ge(o_out, STEPS)
                if tt >= 4:
                    pe.wait_ge(x1_lo, tt - 3)
                for c in range(C):
                    last = nc.tensor.transpose(bank[3 + tt % 4][:, c * P:(c + 1) * P], x1[:, tt, c * P:(c + 1) * P],
                                               identity[:, :])
                last.then_inc(x1_t, 1)

            pe.wait_ge(zeros_set, 1)
            for _ in range(WARM_UP):
                mm(bank[7][:, :], zeros[:, 0:P], zeros[:, :], True, True)
            qkv(0, 1)
            qkv(2)
            pe.wait_ge(consts, 11)
            pe.wait_ge(q_biased, 1)
            pe.wait_ge(kv_biased, 1)
            transpose_stacks(0)
            pe.wait_ge(q_biased, 3)
            pe.wait_ge(kv_biased, 3)
            transpose_stacks(1)
            qkv(3)
            for i in range(STEPS + LAGT):
                behind = max(qkv_behind.get(i - 1, 0), stacks_behind.get(i - 1, 0)) >= TTH and i > LAG2
                if i < STEPS:
                    scores0(i)
                    if behind:
                        scores_t(i - LAG2)
                    scores1(i)
                if i and i % UNIT == 0 and i < STEPS:
                    transpose_maxima(i // UNIT - 1)
                    max_transposed[0] = i // UNIT
                if LAG2 <= i < STEPS + LAG2 and not behind:
                    scores_t(i - LAG2)
                if i == STEPS:
                    transpose_maxima(i // UNIT - 1)
                    max_transposed[0] = i // UNIT
                if LAGV <= i < STEPS + LAGV:
                    pv(i - LAGV)
                if i == STEPS:
                    transpose_ot(0)
                if i == STEPS + LAGT - 1:
                    transpose_x1(0)
                if i >= LAGT:
                    transpose_o(i - LAGT)
                if i in project_behind and project_behind[i] + 1 < TT - 2:
                    transpose_ot(project_behind[i] + 1)
                if i in qkv_behind:
                    if qkv_behind[i] >= 6:
                        pe.wait_ge(max0, i + 1)
                        pe.wait_ge(max1, 2 * (i + 1))
                    elif qkv_behind[i] == 4:
                        pe.wait_ge(kv_biased, 4)
                    else:
                        wait_copied(3)
                    qkv(qkv_behind[i])
                if i in stacks_behind:
                    tt = stacks_behind[i]
                    if tt >= TTH:
                        pe.wait_ge(max0, i + 1)
                        pe.wait_ge(max1, 2 * (i + 1))
                    else:
                        wait_copied(tt - 1)
                    transpose_stacks(tt)
                if i in project_behind:
                    project(project_behind[i])
            transpose_x1(1)
            for tt in range(TT - 2, TT):
                transpose_ot(tt)
            transpose_x1(2)
            transpose_x1(3)
            project(TT - 2)
            project(TT - 1)

            def gate_up(k, unit, between=None):
                slot, tok = k // 2, slice(k % 2 * HALF, k % 2 * HALF + HALF)
                for m, (free, done) in enumerate(((silu_done, gate_done), (val_done, up_done))):
                    if unit is not None:
                        pe.wait_ge(free, unit - 3)
                    o = bank[2 * k + m][:, :]
                    for c in range(C):
                        mm(o, guh[:, slot, m, c, :], x1h[:, c, tok], c == 0, False)
                        mm(o, guh[:, slot, m, c, :], x1l[:, c, tok], False, False)
                        last = mm(o, gul[:, slot, m, c, :], x1h[:, c, tok], False, c == C - 1)
                        if between and (m, c) == (1, 1):
                            between()
                    last.then_inc(done, 1)

            def transpose_second_half():
                for tt in range(TTH, TT):
                    transpose_x1(tt)

            for k in range(4):
                if k < 2:
                    pe.wait_ge(x1_hi, TTH * (k + 1))
                    pe.wait_ge(x1_lo, TTH * (k + 1))
                if k == 0:
                    pe.wait_ge(ot_lo, TT)
                    pe.wait_ge(y_done, TT - 1)
                if k == 1:
                    pe.wait_ge(y_done, TT)
                if k % 2 == 0:
                    pe.wait_ge(gu_hi, k // 2 + 1)
                    pe.wait_ge(gu_lo, k // 2 + 1)
                gate_up(k, None, transpose_second_half if k == 0 else None)
            with pe.Fori(1, PAIRED) as i:
                for k in range(4):
                    if k % 2 == 0:
                        pe.wait_ge(gu_hi, 2 * i + (k // 2 + 1))
                        pe.wait_ge(gu_lo, 2 * i + (k // 2 + 1))
                    gate_up(k, 4 * i + k)
            pe.wait_ge(gu_hi, I_TILES)
            pe.wait_ge(gu_lo, I_TILES)
            for k in range(2):
                gate_up(k, 4 * PAIRED + k)

            pe.wait_ge(val_done, 2 * I_TILES - 2)
            pe.wait_ge(wd_hi, I_TILES)
            pe.wait_ge(wd_lo, I_TILES)
            for n in range(TT + 1):
                tt, half, cols, o = down_part(n)
                if 4 <= n < TT:
                    pe.wait_ge(var2_done, tt - 3)
                tok = slice(tt * P, (tt + 1) * P)
                for t in range(I_TILES):
                    if n % TTH == 0 and t >= I_TILES - 2:
                        pe.wait_ge(inter_done, min(2 * t + 1 + n // TTH, 2 * I_TILES))
                    mm(o, inter_q[:, t, tok], wdh[:, t, cols], t == 0, False)
                    last = mm(o, inter_q[:, t, tok], wdl[:, t, cols], False, t == I_TILES - 1)
                last.then_inc(down_done, 1)

        @block.scalar
        def _(act):
            def split_x(chunks, tok):
                nc.scalar.copy(xh[:, chunks, tok], x_raw[:, chunks, tok]).then_inc(x_hi, 1)

            for c in range(C):
                act.wait_ge(w_in[c], 16)
                nc.scalar.copy(wh[:, c, :], w_raw[:, c, :]).then_inc(w_hi, 1)
                act.wait_ge(x_in[c], 16)
                split_x(c, slice(0, T))
            act.wait_ge(x_batch1_in, 16)
            split_x(slice(0, C), slice(T, HALF))

            def stack_hi(tt):
                par = tt % 2
                if tt >= 2:
                    act.wait_ge(stack_t, TR * (tt - 1))
                else:
                    act.wait_ge(consts, 11)
                act.wait_ge(q_biased, tt + 1)
                q = qkv_rows[:, par, 0:D].rearrange("p (h d) -> p h d", d=HD)
                nc.scalar.copy(q_stack[:, par, :, 0:2 * HD].rearrange("p h (r d) -> p h r d", d=HD).bitcast(F32R),
                               q.unsqueeze(2).to_broadcast([P, H, 2, HD])).then_inc(q_hi, 1)
                act.wait_ge(kv_biased, tt + 1)
                k = qkv_rows[:, par, D:D + KVD].rearrange("p (h d) -> p h d", d=HD)
                nc.scalar.copy(k_stack[:, par].rearrange("p h (r d) -> p h r d", d=HD)[:, :, 0:4:2, :].bitcast(F32R),
                               k.unsqueeze(2).to_broadcast([P, KV, 2, HD])).then_inc(k_hi, 1)

            def copy_stacks(tt):
                for j in copied_by(tt)[0]:
                    act.wait_ge(stack_t, TR * tt + j + 1)
                    out_of_bank(nc.scalar.copy, tt, j, t_act, 0)

            def o_hi(tt):
                act.wait_ge(ot_done, tt + 1)
                if tt >= 2:
                    act.wait_ge(wo_done, tt - 1)
                nc.scalar.copy(oh[:, tt % 2].rearrange("p c q -> p (c q)"), bank[ot_bank(tt)][:, :]).then_inc(ot_hi, 1)

            def probabilities(e):
                p = probs[:, e % 2]
                for a in range(3):
                    act.wait_ge(st_done, 3 * e + a + 1)
                    if a == 0 and e >= 2:
                        act.wait_ge(pv_done, e - 1)
                    if a < 2:
                        dst = p[:, 0:3:2, a:REP:2, :].rearrange("p c h q -> p h c q")
                        src = bank[3 + a][:, :].rearrange("p (h c q) -> p h c q", h=2, c=2)
                    else:
                        dst = p[:, 1].rearrange("p (c a) q -> p a c q", a=2)
                        src = bank[5][:, :].rearrange("p (a c q) -> p a c q", a=2, c=2)
                    nc.scalar.activation(dst, src, ACT.Exp, scale=SCALE).then_inc(exp_done, 1)

            def copy_o(e):
                act.wait_ge(pv_done, e + 1)
                if e >= 2:
                    act.wait_ge(o_t, e - 1)
                nc.scalar.copy(o_cols[:, e % 2, :], bank[6][:, 0:T]).then_inc(o_out, 1)

            def split_gate_up(slot, free=None):
                if free is not None:
                    act.wait_ge(up_done, free)
                nc.scalar.copy(guh[:, slot], gu_raw[:, slot]).then_inc(gu_hi, 1)

            def deviation(first, last, var, done):
                act.wait_ge(var, last)
                nc.scalar.activation(std[:, first:last], mean_var[:, first:last, 1], ACT.Sqrt,
                                     bias=eps_col[:, 0:1]).then_inc(done, 1)

            stack_hi(0)
            stack_hi(1)
            copy_stacks(0)
            copy_stacks(1)
            stack_hi(2)
            stack_hi(3)
            for i in range(STEPS + LAGT):
                if i in project_behind:
                    o_hi(project_behind[i])
                if LAG2 <= i < STEPS + LAG2:
                    probabilities(i - LAG2)
                if i == STEPS + LAGV - 1:
                    deviation(0, TTH, var_done, std_done)
                if LAGV <= i < STEPS + LAGV:
                    copy_o(i - LAGV)
                if i in qkv_behind:
                    stack_hi(qkv_behind[i])
                if i in stacks_behind:
                    copy_stacks(stacks_behind[i])
                    if stacks_behind[i] == TT - 1:
                        act.dma_start(wo_raw[:, :, :], w_o.rearrange("(c p) n -> p c n", p=P)).then_inc(wo_in, 16)
                        act.dma_start(x1[:, :, :], x_tok.rearrange("(t p) d -> p t d", p=P)).then_inc(x1_in, 16)
                if i == 0:
                    act.wait_ge(x2_in, 16)
                    act.wait_ge(kv_done, TTH)
                    for c in range(C):
                        split_x(c, slice(0, HALF))
                if i in WO_AT:
                    if i == WO_AT[0]:
                        act.wait_ge(wo_in, 16)
                    nc.scalar.copy(woh[:, i - WO_AT[0], :], wo_raw[:, i - WO_AT[0], :]).then_inc(wo_hi, 1)
                if i in GU_AT:
                    act.wait_ge(raw_in[i - GU_AT[0]], 32)
                    split_gate_up(i - GU_AT[0])


            def x1_high(tt):
                act.wait_ge(x1_t, tt + 1)
                nc.scalar.copy(x1h[:, :, tt * P:(tt + 1) * P],
                               bank[3 + tt % 4][:, :].rearrange("p (c q) -> p c q", c=C)).then_inc(x1_hi, 1)

            act.wait_ge(o_out, STEPS)
            for tt in range(TT - 2, TT):
                o_hi(tt)
            for tt in range(TTH):
                x1_high(tt)
            deviation(TTH, TT, var_done, std_done)
            for tt in range(TTH, TT):
                x1_high(tt)

            def split_down(t, slot):
                nc.scalar.copy(wdh[:, t, :], wd_raw[:, slot, :]).then_inc(wd_hi, 1)

            def silu_sign(k, unit):
                act.wait_ge(gate_done, unit + 1)
                if not (isinstance(unit, int) and unit < 2):
                    act.wait_ge(inter_done, unit - 1)
                nc.scalar.activation(silu_g[:, k % 2, :], bank[2 * k][:, :], ACT.Silu, scale=1.0 / 128).then_inc(silu_done, 1)
                act.wait_ge(val_done, unit + 1)
                nc.scalar.activation(sign[:, k % 2, :], val[:, k % 2, :], ACT.Sign).then_inc(sign_done, 1)

            act.wait_ge(wo_done, TT)
            for t in range(2):
                split_down(t, t)
            for k in range(4):
                silu_sign(k, k)
                if k % 2:
                    act.wait_ge(raw_in[k // 2], 64)
                    split_gate_up(k // 2, k + 1)
                    split_down(k // 2 + 2, k // 2)
            with act.Fori(1, PAIRED - 1) as i:
                for k in range(4):
                    silu_sign(k, 4 * i + k)
                    if k % 2:
                        act.wait_ge(raw_in[k // 2], 32 * i + 64)
                        split_gate_up(k // 2, 4 * i + (k + 1))
                        split_down(2 * i + (k // 2 + 2), k // 2)
            for k in range(4):
                silu_sign(k, 4 * (PAIRED - 1) + k)
                if k == 1:
                    act.wait_ge(raw_in[0], 32 * (PAIRED + 1))
                    split_gate_up(0, 4 * (PAIRED - 1) + 2)
                    split_down(I_TILES - 1, 0)
            for k in range(2):
                silu_sign(k, 4 * PAIRED + k)

            for n in range(TT + 1):
                tt, half, cols, src = down_part(n)
                act.wait_ge(dmag_done, n + 1)
                if tt >= 2 and half == 0:
                    act.wait_ge(var2_done, tt - 1)
                nc.scalar.activation(sign[:, tt % 2, cols], src, ACT.Sign).then_inc(dsign_done, 1)
                if 1 <= n < TT:
                    act.wait_ge(shift_done, n)
                    nc.scalar.activation(y[:, (n - 1) % 2, :], y[:, (n - 1) % 2, :], ACT.Identity, bias=shift[:, n - 1:n],
                                         scale=rstd[:, n - 1:n]).then_inc(out_done, 1)
                if n != TT - 1:
                    deviation(tt, tt + 1, var2_done, std2_done)

        @block.vector
        def _(dve):
            steps = [0]

            def then(ins, base=0):
                ins.then_inc(dve_step, 1)
                steps[0] += 1
                dve.wait_ge(dve_step, base + steps[0])

            def split_x(n, chunks, tok):
                dve.wait_ge(x_hi, n + 1)
                nc.vector.tensor_tensor(xl[:, chunks, tok], x_raw[:, chunks, tok], xh[:, chunks, tok].bitcast(F32),
                                        ALU.subtract).then_inc(x_lo, 1)

            for c in range(C):
                dve.wait_ge(w_hi, c + 1)
                nc.vector.tensor_tensor(wl[:, c, :], w_raw[:, c, :], wh[:, c, :].bitcast(F32), ALU.subtract).then_inc(w_lo, 1)
                split_x(c, c, slice(0, T))
            split_x(C, slice(0, C), slice(T, HALF))
            dve.wait_ge(bias_in, 32)

            def bias_qkv(tt):
                par = tt % 2
                if tt >= 2:
                    dve.wait_ge(q_lo, tt - 1)
                    dve.wait_ge(k_lo, tt - 1)
                dve.wait_ge(q_done, tt + 1)
                nc.vector.tensor_tensor(qkv_rows[:, par, 0:D], bank[qkv_banks(tt)[0]][:, :], bqkv_rows[:, 0:D],
                                        ALU.add).then_inc(q_biased, 1)
                dve.wait_ge(kv_done, tt + 1)
                nc.vector.tensor_tensor(qkv_rows[:, par, D:QKV], bank[qkv_banks(tt)[1]][:, 0:2 * KVD], bqkv_rows[:, D:QKV],
                                        ALU.add).then_inc(kv_biased, 1)
                dve.wait_ge(kv_biased, tt + 1)
                nc.vector.tensor_copy(v_ones[:, tt, :, 0:HD],
                                      qkv_rows[:, par, D + KVD:QKV].rearrange("p (h d) -> p h d", d=HD)).then_inc(v_in, 1)

            def copy_stacks(tt):
                if tt == 0:
                    dve.wait_ge(consts, 11)
                for j in copied_by(tt)[1]:
                    dve.wait_ge(stack_t, TR * tt + j + 1)
                    out_of_bank(nc.vector.tensor_copy, tt, j, t_dve, 1)

            def maxima0(s):
                u, v = s // UNIT % 2, s % UNIT
                if s // UNIT >= 2 and v == 0:
                    dve.wait_ge(max_t, s // UNIT - 1)
                dve.wait_ge(s0_done, s + 1)
                nc.vector.tensor_reduce(neg_max[:, u, 0, REP * v:REP * (v + 1)],
                                        bank[0][:, :].rearrange("p (h k) -> p h k", h=REP),
                                        AX.X, ALU.max, negate=True).then_inc(max0, 1)

            def maxima1(s):
                u, v = s // UNIT % 2, s % UNIT
                for a in range(2):
                    dve.wait_ge(s1_done, 2 * s + a + 1)
                    nc.vector.tensor_reduce(neg_max[:, u, 1, REP * v + 2 * a:REP * v + 2 * a + 2],
                                            bank[1 + a][:, :].rearrange("p (h k) -> p h k", h=2),
                                            AX.X, ALU.max, negate=True).then_inc(max1, 1)

            def split_maxima(m):
                dve.wait_ge(max_t, m + 1)
                if m >= 2:
                    dve.wait_ge(max_in, 64 * (m - 1))
                nc.vector.tensor_copy(max_rows[:, m % 2, 0, :], bank[7][0:UH, 0:T]).then_inc(max_hi, 1)
                dve.wait_ge(max_hi, m + 1)
                nc.vector.tensor_tensor(max_rows[:, m % 2, 1, :], bank[7][0:UH, 0:T],
                                        max_rows[:, m % 2, 0, :].bitcast(F32), ALU.subtract).then_inc(max_lo, 1)

            def normalise_o(e):
                b, g, _ = at(e)
                o = bank[7][:, 0:2 * P].rearrange("p (t h r) -> p t h r", t=2, h=REP)
                dve.wait_ge(o_t, e + 1)
                nc.vector.reciprocal(inv_sum[:, :, :], o[:, :, :, HD]).then_inc(sum_inv, 1)
                dve.wait_ge(sum_inv, e + 1)
                nc.vector.tensor_tensor(
                    o_tok[:, 2 * b:2 * b + 2, g * REP * HD:(g + 1) * REP * HD].rearrange("p t (h d) -> p t h d", d=HD),
                    o[:, :, :, 0:HD], inv_sum[:, :, :].unsqueeze(3).to_broadcast([P, 2, REP, HD]),
                    ALU.mult).then_inc(o_norm, 1)

            def o_lo(tt):
                dve.wait_ge(ot_hi, tt + 1)
                nc.vector.tensor_tensor(ol[:, tt % 2].rearrange("p c q -> p (c q)"), bank[ot_bank(tt)][:, :],
                                        oh[:, tt % 2].rearrange("p c q -> p (c q)").bitcast(F32),
                                        ALU.subtract).then_inc(ot_lo, 1)

            def add_residual(tt):
                dve.wait_ge(wo_done, tt + 1)
                dve.wait_ge(x_bo, tt + 1)
                nc.vector.tensor_tensor(x1[:, tt, :], bank[1 + tt % 2][:, :], x1[:, tt, :], ALU.add).then_inc(y_done, 1)

            def attention_moments(tt):
                dve.wait_ge(y_done, tt + 1)
                moments(x1[:, tt, :], tt, var_done)

            def moments(y, n, done):
                then(nc.vector.bn_stats(stats[:, 0, :], y))
                nc.vector.bn_aggr(mean_var[:, n, :], stats[:, 0, :]).then_inc(done, 1)

            def normalise(dst, y, n, done):
                nc.vector.tensor_scalar(dst, y, mean_var[:, n, 0:1], rstd[:, n:n + 1],
                                        ALU.subtract, ALU.mult).then_inc(done, 1)

            def low_x1(n):
                tok = slice(n * P, (n + 1) * P)
                dve.wait_ge(x1_hi, n + 1)
                nc.vector.tensor_tensor(x1l[:, :, tok], bank[3 + n % 4][:, :].rearrange("p (c q) -> p c q", c=C),
                                        x1h[:, :, tok].bitcast(F32), ALU.subtract).then_inc(x1_lo, 1)

            for tt in range(3):
                bias_qkv(tt)
            copy_stacks(0)
            copy_stacks(1)
            bias_qkv(3)
            for i in range(STEPS + LAGT):
                if i < STEPS:
                    maxima0(i)
                if i and i % UNIT == 0 and i <= STEPS:
                    split_maxima(i // UNIT - 1)
                if i in project_behind:
                    o_lo(project_behind[i])
                if i < STEPS:
                    maxima1(i)
                if i == STEPS + LAGT - 2:
                    dve.wait_ge(std_done, 1)
                    then(nc.vector.reciprocal(rstd[:, 0:TTH], std[:, 0:TTH]))
                    normalise(x1[:, 0, :], x1[:, 0, :], 0, x1_done)
                if i >= LAGT:
                    normalise_o(i - LAGT)
                if i == STEPS + LAGT - 2:
                    normalise(x1[:, 1, :], x1[:, 1, :], 1, x1_done)
                if i in qkv_behind:
                    bias_qkv(qkv_behind[i])
                if i in stacks_behind:
                    copy_stacks(stacks_behind[i])
                if i - 1 in project_behind and project_behind[i - 1] < TT - 3:
                    add_residual(project_behind[i - 1])
                    attention_moments(project_behind[i - 1])
            for tt in range(2, TTH):
                normalise(x1[:, tt, :], x1[:, tt, :], tt, x1_done)
            o_lo(TT - 2)
            o_lo(TT - 1)
            add_residual(TT - 3)
            for tt in range(TTH):
                low_x1(tt)
            attention_moments(TT - 3)
            for tt in range(TT - 2, TT):
                add_residual(tt)
                attention_moments(tt)
            dve.wait_ge(std_done, 2)
            then(nc.vector.reciprocal(rstd[:, TTH:TT], std[:, TTH:TT]))
            for tt in range(TTH, TT):
                normalise(x1[:, tt, :], x1[:, tt, :], tt, x1_done)
            for tt in range(TTH, TT):
                low_x1(tt)

            def magnitude(k, src, cols=slice(0, BANK)):
                return nc.vector.tensor_scalar(mag[:, k, cols].bitcast(I32), src.bitcast(I32), ABS_12_BITS, None,
                                               ALU.bitwise_and)

            def floor_magnitude(k, base=0, cols=slice(0, BANK)):
                then(nc.vector.tensor_scalar(floor_mag[:, k, cols], mag[:, k, cols], TRUNC_OFFSET, 128.0, ALU.subtract, ALU.min), base)

            def quantise(k, t, unit, base=0):
                dve.wait_ge(up_done, unit + 1)
                dve.wait_ge(silu_done, unit + 1)
                nc.vector.tensor_tensor(val[:, k % 2, :], silu_g[:, k % 2, :], bank[2 * k + 1][:, :], ALU.mult).then_inc(val_done, 1)
                dve.wait_ge(val_done, unit + 1)
                then(magnitude(k % 2, val[:, k % 2, :]), base)
                floor_magnitude(k % 2, base)
                dve.wait_ge(sign_done, unit + 1)
                then(nc.vector.tensor_tensor(q_int[:, k % 2, :], floor_mag[:, k % 2, :], sign[:, k % 2, :], ALU.mult), base)
                nc.vector.tensor_scalar(inter_q[:, t, k % 2 * HALF:(k % 2 + 1) * HALF], q_int[:, k % 2, :], 127.0, 128.0,
                                        ALU.min, ALU.mult).then_inc(inter_done, 1)

            for k in range(4):
                quantise(k, k // 2, k)
            before = steps[0]
            PER_PAIR = 4 * 3
            with dve.Fori(1, PAIRED - 1) as i:
                for k in range(4):
                    quantise(k, 2 * i + k // 2, 4 * i + k, PER_PAIR * i - PER_PAIR)
            assert steps[0] == before + PER_PAIR
            steps[0] = before + PER_PAIR * (PAIRED - 2)
            for k in range(4):
                quantise(k, 2 * (PAIRED - 1) + k // 2, 4 * (PAIRED - 1) + k)
            for k in range(2):
                quantise(k, I_TILES - 1, 4 * PAIRED + k)

            def add_down(n):
                tt, half, cols, src = down_part(n)
                k = tt % 2
                dve.wait_ge(down_done, n + 1)
                magnitude(k, src, cols).then_inc(dmag_done, 1)
                if 1 <= n < TT:
                    dve.wait_ge(std2_done, n)
                    then(nc.vector.reciprocal(rstd[:, n - 1:n], std[:, n - 1:n]))
                    nc.vector.scalar_tensor_tensor(out=shift[:, n - 1:n], in0=mean_var[:, n - 1, 0:1], scalar=-1.0,
                                                   in1=rstd[:, n - 1:n], op0=ALU.mult, op1=ALU.mult).then_inc(shift_done, 1)
                dve.wait_ge(dmag_done, n + 1)
                floor_magnitude(k, 0, cols)
                dve.wait_ge(dsign_done, n + 1)
                then(nc.vector.tensor_tensor(q_int[:, k, cols], floor_mag[:, k, cols], sign[:, k, cols], ALU.mult))
                if tt >= 2 and half == 0:
                    dve.wait_ge(stored[k], 16 * (tt // 2))
                then(nc.vector.scalar_tensor_tensor(out=y[:, k, cols], in0=q_int[:, k, cols], scalar=127.0,
                                                    in1=x1[:, tt, cols], op0=ALU.min, op1=ALU.add))
                then(nc.vector.bn_stats(stats[:, half, :], y[:, k, cols]))

            for tt in range(TT):
                k = tt % 2
                add_down(tt)
                if tt == TT - 1:
                    add_down(TT)
                nc.vector.bn_aggr(mean_var[:, tt, :], stats[:, 0:1 + tt // (TT - 1), :]).then_inc(var2_done, 1)
            dve.wait_ge(std2_done, TT)
            then(nc.vector.reciprocal(rstd[:, tt:tt + 1], std[:, tt:tt + 1]))
            normalise(y[:, k, :], y[:, k, :], tt, last_out_done)


def kernel(L0_attn_x, L0_attn_Wq, L0_attn_bq, L0_attn_Wk, L0_attn_bk, L0_attn_Wv, L0_attn_bv, L0_attn_Wo, L0_attn_bo,
           L0_ffn_w_gate, L0_ffn_w_up, L0_ffn_w_down):
    import numpy as np
    import concourse.bacc as bacc
    from concourse.bass_utils import run_bass_kernel_spmd

    x = np.asarray(L0_attn_x)
    batches, tokens, width = x.shape
    x_tok = x.reshape(batches * tokens, width)
    gate, up, down = (np.asarray(w) for w in (L0_ffn_w_gate, L0_ffn_w_up, L0_ffn_w_down))
    inner = gate.shape[0]
    tiles = -(-inner // P)
    chunks = width // P

    def inner_tiles(w):
        padded = np.zeros((tiles * P, width), w.dtype)
        padded[:inner] = w
        return padded.reshape(tiles, P, chunks, P).transpose(0, 3, 2, 1)

    down_t = np.zeros((tiles * P, width), down.dtype)
    down_t[:inner] = down.T
    arrays = {
        "xT": x_tok.T,
        "x_tok": x_tok,
        "w_qkv": np.concatenate([np.asarray(w) for w in (L0_attn_Wq, L0_attn_Wk, L0_attn_Wv)], axis=1),
        "b_qkv": np.concatenate([np.asarray(b) for b in (L0_attn_bq, L0_attn_bk, L0_attn_bv)]),
        "w_o": np.asarray(L0_attn_Wo),
        "b_o": np.asarray(L0_attn_bo),
        "w_gate_up": np.stack([inner_tiles(gate), inner_tiles(up)], axis=2),
        "w_down": down_t.reshape(tiles, P, width),
    }
    arrays = {name: np.ascontiguousarray(a) for name, a in arrays.items()}
    nc = bacc.Bacc("TRN2", target_bir_lowering=False, num_devices=1)
    args = [nc.dram_tensor(name, a.shape, mybir.dt.from_np(a.dtype), kind="ExternalInput").ap() for name, a in arrays.items()]
    args.append(nc.dram_tensor("out", x_tok.shape, mybir.dt.from_np(x_tok.dtype), kind="ExternalOutput").ap())
    layer(nc, *args)
    got = run_bass_kernel_spmd(nc, [arrays], core_ids=[0]).results[0]["out"]
    return got.reshape(x.shape)
```
